# Optimizing a Trainium2 kernel written in Bass

```python
import numpy as np
import jax
import jax.numpy as jnp

def _softmax(x, axis=-1):
    return jax.nn.softmax(x, axis=axis)

def _gelu(x):
    return jax.nn.gelu(x, approximate=True)

def _silu(x):
    return jax.nn.silu(x)

def _sigmoid(x):
    return jax.nn.sigmoid(x)

def _layernorm(x, axis=-1, eps=1e-05):
    m = jnp.mean(x, axis=axis, keepdims=True)
    v = jnp.var(x, axis=axis, keepdims=True)
    return (x - m) / jnp.sqrt(v + eps)

def _scatter_add(tgt, idx, src, axis=0):
    return tgt.at[idx].add(src)

def _segment_sum(src, seg, n):
    return jax.ops.segment_sum(src, seg, n)
kernel_name = 'mk_early_fusion_embed_d1_tok_img256_r4_d23538'

def setup_inputs(seed: int=0):
    np.random.seed(seed)
    _w = jnp.asarray

    def _rec_inputs():
        import jax
        import jax.numpy as jnp
        _rk = jax.random.key(seed)
        x = -7.10856e-05 + 0.999911 * jax.random.normal(jax.random.fold_in(_rk, 1), (64, 1, 128, 128), jnp.float32)
        x_txt = jax.random.randint(jax.random.fold_in(_rk, 51), (64, 32), 0, 2048, jnp.int32)
        return (x, x_txt)
    x, x_txt = _rec_inputs()

    def _L0_tok_setup():
        import jax, jax.numpy as jnp
        import numpy as np
        INV_SQRT2 = 0.7071067811865476

        def haar_dwt2(x):
            lo = (x[..., ::2] + x[..., 1::2]) * INV_SQRT2
            hi = (x[..., ::2] - x[..., 1::2]) * INV_SQRT2
            cA = (lo[..., ::2, :] + lo[..., 1::2, :]) * INV_SQRT2
            cH = (lo[..., ::2, :] - lo[..., 1::2, :]) * INV_SQRT2
            cV = (hi[..., ::2, :] + hi[..., 1::2, :]) * INV_SQRT2
            cD = (hi[..., ::2, :] - hi[..., 1::2, :]) * INV_SQRT2
            return (cA, (cH, cV, cD))

        def wavedec2_maps(x, levels):
            a = x
            details = []
            for _ in range(levels):
                a, d = haar_dwt2(a)
                details.append(d)
            maps = [a]
            for d in reversed(details):
                maps.extend(d)
            return maps
        key = jax.random.key(seed)
        k1, k2 = jax.random.split(key)
        B, H, W_img = (64, 256, 256)
        x = jax.random.normal(k1, (B, 1, H, W_img), dtype=jnp.float32)
        n_maps = 1 + 3 * 2
        W = jax.random.normal(k2, (n_maps, 64), dtype=jnp.float32) * (1.0 / np.sqrt(n_maps))
        b = jnp.zeros((64,), dtype=jnp.float32)
        return {'x': x, 'W': W, 'b': b}
    _L0_tok_all = _L0_tok_setup()
    _L0_tok_in = {k: v for k, v in _L0_tok_all.items() if k in ('W', 'b')}
    del _L0_tok_all

    def _L0_txt_setup():
        import jax, jax.numpy as jnp
        import numpy as np
        D = 64
        NLEAF = 8
        N_INTERNAL = 7
        N_STRUCT = 2048
        COMP_V = 256
        OP_V = 64
        EPS = 1e-05

        def _layer_norm(x, gamma, beta):
            mu = jnp.mean(x, axis=-1, keepdims=True)
            var = jnp.mean(jnp.square(x - mu), axis=-1, keepdims=True)
            return (x - mu) * jax.lax.rsqrt(var + EPS) * gamma + beta
        key = jax.random.key(seed)
        ks = jax.random.split(key, 8)
        struct_indices = jax.random.randint(ks[0], (32, 512), 0, N_STRUCT)
        leaf_ids = jax.random.randint(ks[1], (N_STRUCT, NLEAF), 0, COMP_V).astype(jnp.int32)
        op_ids = jax.random.randint(ks[2], (N_STRUCT, N_INTERNAL), 0, OP_V).astype(jnp.int32)
        comp_emb = jax.random.normal(ks[3], (COMP_V, D), dtype=jnp.float32)
        op_emb = jax.random.normal(ks[4], (OP_V, D), dtype=jnp.float32)
        W_bin = jax.random.normal(ks[5], (3 * D, D), dtype=jnp.float32) / np.sqrt(3 * D)
        b_bin = jnp.zeros((D,), dtype=jnp.float32)
        gamma = jnp.ones((D,), dtype=jnp.float32)
        beta = jnp.zeros((D,), dtype=jnp.float32)
        return {'struct_indices': struct_indices, 'leaf_ids': leaf_ids, 'op_ids': op_ids, 'comp_emb': comp_emb, 'op_emb': op_emb, 'W_bin': W_bin, 'b_bin': b_bin, 'gamma': gamma, 'beta': beta}
    _L0_txt_all = _L0_txt_setup()
    _L0_txt_in = {k: v for k, v in _L0_txt_all.items() if k in ('leaf_ids', 'op_ids', 'comp_emb', 'op_emb', 'W_bin', 'b_bin', 'gamma', 'beta')}
    del _L0_txt_all

    def _L0_attn_setup():
        import jax, jax.numpy as jnp
        import numpy as np
        KERNEL_SIZE = 3
        DILATIONS = (1, 2, 3)

        def _window(t, dilation, ksize):
            B, N, C = t.shape
            pad = dilation * (ksize - 1) // 2
            tp = jnp.pad(t, ((0, 0), (pad, pad), (0, 0)))
            idx = jnp.arange(N)[:, None] + jnp.arange(ksize)[None, :] * dilation
            return tp[:, idx, :]
        key = jax.random.key(seed)
        k0, k1, k2 = jax.random.split(key, 3)
        B, N, C = (16, 1024, 64)
        x = jax.random.normal(k0, (B, N, C), jnp.float32)
        Wqkv = jax.random.normal(k1, (len(DILATIONS), C, 3 * C), jnp.float32) * 0.02
        Wproj = jax.random.normal(k2, (C, C), jnp.float32) * 0.02
        bproj = jnp.zeros((C,), jnp.float32)
        return {'x': x, 'Wqkv': Wqkv, 'Wproj': Wproj, 'bproj': bproj}
    _L0_attn_all = _L0_attn_setup()
    _L0_attn_in = {k: v for k, v in _L0_attn_all.items() if k in ('Wqkv', 'Wproj', 'bproj')}
    del _L0_attn_all

    def _L0_ffn_setup():
        import jax, jax.numpy as jnp
        import numpy as np
        E = 8
        K = 2
        D = 64
        H = 128
        DOUT = 64
        EPS = 1e-05
        key = jax.random.key(seed)
        ks = jax.random.split(key, 9)
        s = 0.02
        return {'x': jax.random.normal(ks[0], (4, 2048, D), jnp.float32), 'gamma': 1.0 + 0.05 * jax.random.normal(ks[1], (D,), jnp.float32), 'beta': 0.05 * jax.random.normal(ks[2], (D,), jnp.float32), 'Wr': 0.01 * jax.random.normal(ks[3], (D, E), jnp.float32), 'br': jnp.zeros((E,), jnp.float32), 'W1': s * jax.random.normal(ks[4], (E, D, H), jnp.float32), 'b1': s * jax.random.normal(ks[5], (E, H), jnp.float32), 'W2': s * jax.random.normal(ks[6], (E, H, DOUT), jnp.float32), 'b2': s * jax.random.normal(ks[7], (E, DOUT), jnp.float32)}
    _L0_ffn_all = _L0_ffn_setup()
    _L0_ffn_in = {k: v for k, v in _L0_ffn_all.items() if k in ('gamma', 'beta', 'Wr', 'br', 'W1', 'b1', 'W2', 'b2')}
    del _L0_ffn_all
    return {'x': x, 'x_txt': x_txt, 'L0_tok_W': _L0_tok_in['W'], 'L0_tok_b': _L0_tok_in['b'], 'L0_txt_leaf_ids': _L0_txt_in['leaf_ids'], 'L0_txt_op_ids': _L0_txt_in['op_ids'], 'L0_txt_comp_emb': _L0_txt_in['comp_emb'], 'L0_txt_op_emb': _L0_txt_in['op_emb'], 'L0_txt_W_bin': _L0_txt_in['W_bin'], 'L0_txt_b_bin': _L0_txt_in['b_bin'], 'L0_txt_gamma': _L0_txt_in['gamma'], 'L0_txt_beta': _L0_txt_in['beta'], 'L0_attn_Wqkv': _L0_attn_in['Wqkv'], 'L0_attn_Wproj': _L0_attn_in['Wproj'], 'L0_attn_bproj': _L0_attn_in['bproj'], 'L0_ffn_gamma': _L0_ffn_in['gamma'], 'L0_ffn_beta': _L0_ffn_in['beta'], 'L0_ffn_Wr': _L0_ffn_in['Wr'], 'L0_ffn_br': _L0_ffn_in['br'], 'L0_ffn_W1': _L0_ffn_in['W1'], 'L0_ffn_b1': _L0_ffn_in['b1'], 'L0_ffn_W2': _L0_ffn_in['W2'], 'L0_ffn_b2': _L0_ffn_in['b2']}

def reference(x, x_txt, L0_tok_W, L0_tok_b, L0_txt_leaf_ids, L0_txt_op_ids, L0_txt_comp_emb, L0_txt_op_emb, L0_txt_W_bin, L0_txt_b_bin, L0_txt_gamma, L0_txt_beta, L0_attn_Wqkv, L0_attn_Wproj, L0_attn_bproj, L0_ffn_gamma, L0_ffn_beta, L0_ffn_Wr, L0_ffn_br, L0_ffn_W1, L0_ffn_b1, L0_ffn_W2, L0_ffn_b2):
    import jax
    import jax.numpy as jnp

    def _L0_tok_ref(x, W, b):
        import jax, jax.numpy as jnp
        import numpy as np
        INV_SQRT2 = 0.7071067811865476

        def haar_dwt2(x):
            lo = (x[..., ::2] + x[..., 1::2]) * INV_SQRT2
            hi = (x[..., ::2] - x[..., 1::2]) * INV_SQRT2
            cA = (lo[..., ::2, :] + lo[..., 1::2, :]) * INV_SQRT2
            cH = (lo[..., ::2, :] - lo[..., 1::2, :]) * INV_SQRT2
            cV = (hi[..., ::2, :] + hi[..., 1::2, :]) * INV_SQRT2
            cD = (hi[..., ::2, :] - hi[..., 1::2, :]) * INV_SQRT2
            return (cA, (cH, cV, cD))

        def wavedec2_maps(x, levels):
            a = x
            details = []
            for _ in range(levels):
                a, d = haar_dwt2(a)
                details.append(d)
            maps = [a]
            for d in reversed(details):
                maps.extend(d)
            return maps
        imgs = x[:, 0]
        B = imgs.shape[0]
        maps = wavedec2_maps(imgs, 2)
        proc = [jax.image.resize(m, (B, 8, 8), method='bilinear') for m in maps]
        feat = jnp.stack(proc, axis=1)
        feat = feat.reshape(B, feat.shape[1], 64).transpose(0, 2, 1)
        return feat @ W + b

    def _L0_txt_ref(struct_indices, leaf_ids, op_ids, comp_emb, op_emb, W_bin, b_bin, gamma, beta):
        import jax, jax.numpy as jnp
        import numpy as np
        D = 64
        NLEAF = 8
        N_INTERNAL = 7
        N_STRUCT = 2048
        COMP_V = 256
        OP_V = 64
        EPS = 1e-05

        def _layer_norm(x, gamma, beta):
            mu = jnp.mean(x, axis=-1, keepdims=True)
            var = jnp.mean(jnp.square(x - mu), axis=-1, keepdims=True)
            return (x - mu) * jax.lax.rsqrt(var + EPS) * gamma + beta
        h = _layer_norm(comp_emb[leaf_ids], gamma, beta)
        off = 0
        while h.shape[1] > 1:
            n = h.shape[1] // 2
            ops = op_emb[op_ids[:, off:off + n]]
            cat = jnp.concatenate([ops, h[:, 0::2], h[:, 1::2]], axis=-1)
            h = _layer_norm(jnp.einsum('nkc,cd->nkd', cat, W_bin) + b_bin, gamma, beta)
            off += n
        root = h[:, 0]
        out = root[struct_indices]
        mask = (struct_indices > 1)[..., None]
        return jnp.where(mask, out, jnp.zeros((), dtype=out.dtype))

    def _L0_attn_ref(x, Wqkv, Wproj, bproj):
        import jax, jax.numpy as jnp
        import numpy as np
        KERNEL_SIZE = 3
        DILATIONS = (1, 2, 3)

        def _window(t, dilation, ksize):
            B, N, C = t.shape
            pad = dilation * (ksize - 1) // 2
            tp = jnp.pad(t, ((0, 0), (pad, pad), (0, 0)))
            idx = jnp.arange(N)[:, None] + jnp.arange(ksize)[None, :] * dilation
            return tp[:, idx, :]
        B, N, C = x.shape
        scale = C ** (-0.5)
        outs = []
        for i, d in enumerate(DILATIONS):
            qkv = x @ Wqkv[i]
            q, k, v = jnp.split(qkv, 3, axis=-1)
            kw = _window(k, d, KERNEL_SIZE)
            vw = _window(v, d, KERNEL_SIZE)
            logits = jnp.einsum('bnc,bnkc->bnk', q, kw) * scale
            attn = jax.nn.softmax(logits, axis=-1)
            outs.append(jnp.einsum('bnk,bnkc->bnc', attn, vw))
        combined = jnp.mean(jnp.stack(outs, axis=0), axis=0)
        return combined @ Wproj + bproj

    def _L0_ffn_ref(x, gamma, beta, Wr, br, W1, b1, W2, b2):
        import jax, jax.numpy as jnp
        import numpy as np
        E = 8
        K = 2
        D = 64
        H = 128
        DOUT = 64
        EPS = 1e-05
        mu = jnp.mean(x, axis=-1, keepdims=True)
        var = jnp.mean(jnp.square(x - mu), axis=-1, keepdims=True)
        xn = (x - mu) * jax.lax.rsqrt(var + EPS) * gamma + beta
        logits = jnp.einsum('bsd,de->bse', xn, Wr) + br
        top_vals, top_idx = jax.lax.top_k(logits, K)
        w = jax.nn.softmax(top_vals, axis=-1)
        w_full = jnp.einsum('bsk,bske->bse', w, jax.nn.one_hot(top_idx, E, dtype=w.dtype))
        y = jnp.zeros(x.shape[:-1] + (DOUT,), x.dtype)
        for e in range(E):
            h = jax.nn.gelu(jnp.einsum('bsd,dh->bsh', xn, W1[e]) + b1[e], approximate=False)
            y_e = jnp.einsum('bsh,hd->bsd', h, W2[e]) + b2[e]
            y = y + y_e * w_full[..., e, None]
        return y
    h = _L0_tok_ref(x, L0_tok_W, L0_tok_b)
    h = jnp.concatenate([h, _L0_txt_ref(x_txt, L0_txt_leaf_ids, L0_txt_op_ids, L0_txt_comp_emb, L0_txt_op_emb, L0_txt_W_bin, L0_txt_b_bin, L0_txt_gamma, L0_txt_beta)], axis=1)
    h = h + _L0_attn_ref(_layernorm(h, axis=-1), L0_attn_Wqkv, L0_attn_Wproj, L0_attn_bproj)
    h = h + _L0_ffn_ref(_layernorm(h, axis=-1), L0_ffn_gamma, L0_ffn_beta, L0_ffn_Wr, L0_ffn_br, L0_ffn_W1, L0_ffn_b1, L0_ffn_W2, L0_ffn_b2)
    return h

_drawn_inputs = setup_inputs


def setup_inputs(seed=0):
    import zlib

    import numpy as np

    out = dict(_drawn_inputs(seed))
    spreads = {'L0_tok_b': (0.0, 0.1),
     'L0_txt_b_bin': (0.0, 0.1),
     'L0_txt_gamma': (1.0, 0.2),
     'L0_txt_beta': (0.0, 0.1),
     'L0_attn_bproj': (0.0, 0.1),
     'L0_ffn_br': (0.0, 0.272)}
    factors = {'L0_attn_Wqkv': 3.105,
     'L0_attn_Wproj': 3.261,
     'L0_ffn_gamma': 8.0,
     'L0_ffn_beta': 8.0,
     'L0_ffn_Wr': 4.761,
     'L0_ffn_W1': 2.715,
     'L0_ffn_b1': 8.0,
     'L0_ffn_W2': 2.787,
     'L0_ffn_b2': 4.601}
    for name, (base, spread) in spreads.items():
        noise = np.random.default_rng([zlib.crc32(name.encode()), seed]).standard_normal(out[name].shape)
        drawn = base * np.exp(spread * noise) if base else spread * noise
        out[name] = jnp.asarray(drawn.astype(out[name].dtype))
    for name, factor in factors.items():
        out[name] = (out[name] * factor).astype(out[name].dtype)
    return out
```

```python
from contextlib import ExitStack

import numpy as np
import concourse.bass as bass
from concourse import mybir

F32 = mybir.dt.float32
F32R = mybir.dt.float32r
BF16 = mybir.dt.bfloat16
I32 = mybir.dt.int32
U32 = mybir.dt.uint32
ALU = mybir.AluOpType
ACT = mybir.ActivationFunctionType
AX = mybir.AxisListType

P = 128
B = 64
D = 64
NTOK = 96
T = NTOK // 2
TXT_T = 16
CH = 4
NCH = T // CH
HALO = 3
DIL = (1, 2, 3)
ND = 3
KW = 3
EPS = 1e-5
EPS2 = EPS * EPS
IMG = 128
NG = 4
G8 = 8 * NG
NLEAF = 8
NOP = 7
NID = 16
SP = 16
TXT = 2048
VB = 512
NE = 8
HID = 128
NEG = -1e30


def ap_of(view, dims):
    return bass.AP(tensor=view.tensor, offset=view.offset, ap=[list(view.ap[0]), *dims])


class Count:

    def __init__(self, sem):
        self.sem, self.base, self.n = sem, 0, 0

    def add(self, ins):
        ins.then_inc(self.sem, 1)
        self.n += 1
        return self.base + self.n

    def enter(self, turns, per):
        self.outer, self.per, self.start = (self.base, self.n), per, self.base + self.n
        self.base, self.n = turns * per + self.start, 0

    def leave(self, turns):
        assert self.n == self.per, (self.n, self.per)
        self.base, self.n = self.start + turns * self.per, 0


def build(nc, x):
    ctx = ExitStack()
    with ctx:
        def sb(name, shape, dt=F32):
            return ctx.enter_context(nc.sbuf_tensor(name, shape, dt))

        def sem(name):
            return ctx.enter_context(nc.semaphore(name))

        PS = ctx.enter_context(nc.psum_tensor("PS", [P, 8, 512], F32))

        ident = sb("ident", [P, P])
        identb = sb("identb", [P, P], BF16)
        gt = sb("gt", [P, G8])
        iota3 = sb("iota3", [P, 3])
        iota8 = sb("iota8", [P, NE])
        ones = sb("ones", [1, P])
        onesb = sb("onesb", [96, P], BF16)
        REG = (T + 2 * HALO) * 2 * ND * D
        reg = sb("reg", [P, REG])
        onehot = reg[:, 0:NLEAF * 2 * TXT // 2].bitcast(BF16).rearrange("p (l n) -> p l n", n=TXT)
        uv = reg[:, :].rearrange("p (t n) -> p t n", n=2 * ND * D)
        img = sb("img", [P, B, IMG])
        onehot_op = img[:, :, :].rearrange("p b w -> p (b w)")[:, 0:NOP * TXT // 2]\
            .bitcast(BF16).rearrange("p (l n) -> p l n", n=TXT)
        imgf = img[:, :, :].rearrange("p b w -> p (b w)")
        taken = [0]

        def late(*shape):
            n = int(np.prod(shape))
            v = imgf[:, taken[0]:taken[0] + n]
            taken[0] += n
            names = "abc"[:len(shape)]
            return v.rearrange(f"p ({' '.join(names)}) -> p {' '.join(names)}", **dict(zip(names, shape)))

        spare = reg[:, NLEAF * TXT:]
        o1 = spare[:, 0:G8 * B].rearrange("p (g b) -> p g b", b=B)
        ya = sb("ya", [P, T, 8])
        yt = sb("yt", [D, 6, P])
        wbd = sb("wbd", [D, 8, D])
        tok = sb("tok", [P, SP], I32)
        idg = sb("idg", [P, SP, NID], I32)
        idb = sb("idb", [P, SP, NID], BF16)
        idsT = spare[0:NID, G8 * B:G8 * B + TXT // 2].bitcast(BF16)
        mask = sb("mask", [P, SP])
        mbeta = spare[:, G8 * B + TXT // 2:G8 * B + TXT // 2 + SP * D].rearrange("p (s d) -> p s d", d=D)
        bcb = sb("bcb", [P, 3, VB], BF16)
        wall = sb("wall", [P, 4, D])
        wsum = sb("wsum", [P, 4])
        wg = sb("wg", [P, 3, D])
        opT = sb("opT", [D, D])
        comp = sb("comp", [P, 2, D])
        zc = sb("zc", [P, 2, D])
        zcT = sb("zcT", [D, 2, P])
        stc = sb("stc", [P, 2, 6])
        mvc = sb("mvc", [P, 2, 2])
        rc = sb("rc", [P, 2])
        tgc = sb("tgc", [P, 1])
        tbc = sb("tbc", [P, 1])
        tgr = sb("tgr", [P, D])
        tbr = sb("tbr", [P, D])
        tabr = sb("tabr", [P, 5 * D])
        tab = sb("tab", [P, 3, 5 * D], BF16)
        opab = sb("opab", [P, 2, D], BF16)
        z1 = sb("z1", [P, 8, D])
        z2 = sb("z2", [P, 4, D])
        z1T = sb("z1T", [P, 4, P])
        z2T_ = sb("z2Tt", [P, 2, P])
        sq = sb("sq", [P, 14, D])
        ss = sb("ss", [P, 14])
        rt = sb("rt", [P, 14])
        fin = sb("fin", [P, 2, D])
        hall = sb("hall", [P, T, D])
        zall = sb("zall", [P, T + 2 * HALO, D])
        zs = late(CH, 2, D)
        zT = sb("zT", [P, CH, P], F32R)
        wqkvT = sb("wqkvT", [D, ND, 3, D])
        wproj = sb("wproj", [D, D])
        bproj = sb("bproj", [P, D])
        mv32 = sb("mv32", [P, 2 * ND * D])
        mvh = sb("mvh", [P, 2 * ND * D], F32R)
        mvl = sb("mvl", [P, 2 * ND * D], F32R)
        st1 = sb("st1", [P, CH, 6])
        mm1 = sb("mm1", [P, CH, 2])
        r1 = sb("r1", [P, CH])
        prod = late(CH * ND * KW * D)
        lg = sb("lg", [P, CH, ND * KW])
        ex = sb("ex", [P, CH, ND * KW])
        at = sb("at", [P, CH, ND * KW])
        mx = sb("mx", [P, CH * ND])
        sm = sb("sm", [P, CH * ND])
        rs = sb("rs", [P, CH * ND])
        av = late(CH, D)
        st2 = sb("st2", [P, CH, 6])
        mm2 = sb("mm2", [P, CH, 2])
        r2 = sb("r2", [P, CH])
        z32 = late(CH, D)
        z2s = late(CH, 2, D)
        z2T = sb("z2T", [P, CH, P], F32R)
        w1 = sb("w1", [P, NE * HID])
        w1h = sb("w1h", [P, NE * HID], F32R)
        w1l = sb("w1l", [P, NE * HID], F32R)
        wr = sb("wr", [P, NE])
        wrh = sb("wrh", [P, NE], F32R)
        wrl = sb("wrl", [P, NE], F32R)
        fgc = sb("fgc", [P, 1])
        fbc = sb("fbc", [P, 1])
        brow = sb("brow", [1, NE])
        br = sb("br", [P, NE])
        b1 = sb("b1", [P, NE])
        w2 = sb("w2", [P, NE, D])
        b2x = sb("b2x", [96, NE * D])
        b2b = sb("b2b", [96, NE * D], BF16)
        b2p = sb("b2p", [96, NE * D], BF16)
        rl = sb("rl", [P, CH, NE])
        v8 = sb("v8", [P, CH, NE])
        i8 = sb("i8", [P, CH, NE], U32)
        i8f = sb("i8f", [P, CH, 2])
        dm = sb("dm", [P, CH])
        th = sb("th", [P, CH])
        tw = sb("tw", [P, CH, 2])
        se1 = sb("se1", [P, CH, NE])
        se2 = sb("se2", [P, CH, NE])
        wf = sb("wf", [P, CH, NE])
        hT = late(2, CH, P)
        yw = late(2, NE, D)
        yo = late(CH, D)

        ld_const = sem("ld_const")
        ld_tok = sem("ld_tok")
        ld_txt = sem("ld_txt")
        ld_att = sem("ld_att")
        ld_ffn = sem("ld_ffn")
        ld_b2 = sem("ld_b2")
        ld_emb = sem("ld_emb")
        ld_img = [sem(f"ld_img{i}") for i in range(4)]
        gathered = sem("gathered")
        zeroed = sem("zeroed")
        consts = sem("consts")
        vec = sem("vec")
        wc_ready = sem("wc_ready")
        vc_ready = sem("vc_ready")
        rc_ready = sem("rc_ready")
        zc_ready = sem("zc_ready")
        zct_done = sem("zct_done")
        zct_saved = sem("zct_saved")
        tab_done = sem("tab_done")
        tab_ready = sem("tab_ready")
        mv_done = sem("mv_done")
        mv_ready = sem("mv_ready")
        bias_done = sem("bias_done")
        ffn_ready = sem("ffn_ready")
        o1_done = sem("o1_done")
        o1_saved = sem("o1_saved")
        y_done = sem("y_done")
        ya_ready = sem("ya_ready")
        yt_done = sem("yt_done")
        yt_saved = sem("yt_saved")
        emb_done = sem("emb_done")
        emb_saved = sem("emb_saved")
        idb_ready = sem("idb_ready")
        idT_done = sem("idT_done")
        idT_saved = sem("idT_saved")
        bc_done = sem("bc_done")
        bc_saved = sem("bc_saved")
        bc_used = sem("bc_used")
        mb_ready = sem("mb_ready")
        mask_ready = sem("mask_ready")
        x_done = [sem(f"x{n}_done") for n in (1, 2, 3)]
        sq_done = [sem(f"sq{n}_done") for n in (1, 2, 3)]
        ss_done = [sem(f"ss{n}_done") for n in (1, 2, 3)]
        rt_done = [sem(f"rt{n}_done") for n in (1, 2, 3)]
        z_done = [sem(f"z{n}_done") for n in (1, 2, 3)]
        zt_done = [sem(f"zt{n}_done") for n in (1, 2)]
        zt_saved = [sem(f"zt{n}_saved") for n in (1, 2)]
        var1 = sem("var1")
        rstd1 = sem("rstd1")
        zs_ready = sem("zs_ready")
        ztp_done = sem("ztp_done")
        zT_ready = sem("zT_ready")
        uv_done = sem("uv_done")
        uv_saved = sem("uv_saved")
        halo_v = sem("halo_v")
        halo_zero = sem("halo_zero")
        hb_ready = sem("hb_ready")
        sm_ready = sem("sm_ready")
        ex_ready = sem("ex_ready")
        var2 = sem("var2")
        rstd2 = sem("rstd2")
        z2s_ready = sem("z2s_ready")
        z2tp_done = sem("z2tp_done")
        z2T_ready = sem("z2T_ready")
        lg_done = sem("lg_done")
        lg_used = sem("lg_used")
        dm_ready = sem("dm_ready")
        th_ready = sem("th_ready")
        h_done = sem("h_done")
        h_saved = sem("h_saved")
        y2_done = sem("y2_done")
        y2_used = sem("y2_used")
        out_ready = sem("out_ready")
        stored = sem("stored")

        col = lambda n, start=0: bass.AP(tensor=x[n].tensor, offset=start, ap=[[1, D], [1, 1]])
        row = lambda n, parts: bass.AP(tensor=x[n].tensor, offset=0, ap=[[0, parts], [1, D]])

        block = ctx.enter_context(nc.Block())

        def apart(eng, s, value, addressed=False):
            if not isinstance(value, int):
                value = eng.snap(eng.to_reg(value))
            for _ in range(1 + addressed):
                eng.wait_ge(zeroed, 1)
            eng.wait_ge(s, value)

        def chunk_of(n):
            if isinstance(n, int):
                return NCH - 1 if n == 0 else n - 1
            return n - 1

        @block.sync
        def _(sp):
            sp.dma_start(tok[:, :], x["tok"]).then_inc(ld_tok, 16)
            sp.dma_start(ident[:, :], x["ident"]).then_inc(ld_const, 16)
            sp.dma_start(gt[:, :], x["gt"]).then_inc(ld_const, 16)
            sp.dma_start(iota3[:, :], x["iota3"]).then_inc(ld_const, 16)
            sp.dma_start(iota8[:, :], x["iota8"]).then_inc(ld_const, 16)
            for i in range(4):
                sp.dma_start(img[:, 16 * i:16 * i + 16, :], x["img"][:, 16 * i:16 * i + 16, :])\
                  .then_inc(ld_img[i], 16)
            sp.dma_start(w1[0:D, :], x["w1"]).then_inc(ld_ffn, 16)
            sp.dma_start(w1[D:P, :], x["w1"]).then_inc(ld_ffn, 16)
            sp.dma_start(w2[:, :, :], x["w2"]).then_inc(ld_ffn, 16)
            for h in range(2):
                sp.dma_start(wr[D * h:D * h + D, :], x["wr"]).then_inc(ld_ffn, 16)
                sp.dma_start(fgc[D * h:D * h + D, :], col("fg")).then_inc(ld_ffn, 16)
                sp.dma_start(fbc[D * h:D * h + D, :], col("fb")).then_inc(ld_ffn, 16)
            sp.dma_start(brow[:, :], x["br"].rearrange("(a n) -> a n", a=1)).then_inc(ld_ffn, 16)
            sp.dma_start(b1[:, :], x["b1"]).then_inc(ld_ffn, 16)
            sp.wait_ge(zeroed, 2)
            for q in range(3):
                sp.dma_start(b2x[32 * q:32 * q + 1, :], x["b2"].rearrange("(a n) -> a n", a=1))\
                  .then_inc(ld_b2, 16)
            o = x["out"].rearrange("b (h t) d -> h b t d", h=2)

            def store(k):
                sp.wait_ge(out_ready, k + 1)
                for h in range(2):
                    sp.dma_start(o[h, :, bass.ds(k * CH, CH), :],
                                 hall[D * h:D * h + D, bass.ds(k * CH, CH), :]).then_inc(stored, 16)

            with sp.Fori(0, NCH) as k:
                store(k)
            sp.wait_ge(stored, 16 * 2 * NCH)

        @block.gpsimd
        def _(pool):
            pool.wait_ge(ld_tok, 16)
            for s in range(SP):
                pool.indirect_dma_start(
                    out=idg[:, s, :], out_offset=None, in_=x["ids"],
                    in_offset=bass.IndirectOffsetOnAxis(ap=tok[:, s:s + 1].bitcast(U32), axis=0))\
                    .then_inc(gathered, 16)
            nh = pool_const = sb("nh", [P, 16])
            pw = sem("pool_step")
            n_pw = Count(pw)

            t = n_pw.add(pool.memset(nh[:, :], -0.5))
            pool.wait_ge(pw, t)

            def root(out, var, scale, add, n, done):
                t = n_pw.add(pool.tensor_scalar(out, var, scale, add, ALU.mult, ALU.add))
                pool.wait_ge(pw, t)
                pool.tensor_tensor(out, out, nh[:, 0:n], ALU.pow).then_inc(done, 1)

            pool.wait_ge(vc_ready, 1)
            root(rc[:, :], mvc[:, :, 1], 1.0, EPS, 2, rc_ready)
            pool.wait_ge(mask_ready, 1)
            pool.wait_ge(ld_txt, TXT_LOADS * 16)
            pool.tensor_tensor(mbeta[:, :, :], mask[:, :].unsqueeze(2).to_broadcast([P, SP, D]),
                               tbr[:, :].unsqueeze(1).to_broadcast([P, SP, D]), ALU.mult).then_inc(mb_ready, 1)

            LV = ((0, 8), (8, 4), (12, 2))

            def text(g, lv):
                a, n = LV[lv]
                apart(pool, ss_done[lv], g - lv + 1)
                root(rt[:, a:a + n], ss[:, a:a + n], 1.0 / D, EPS, n, rt_done[lv])

            text(0, 0)
            text(1, 0)
            text(1, 1)
            n_pw.enter(0, 3)
            first = n_pw.start
            with pool.Fori(2, 8) as g:
                n_pw.base = (g - 2) * 3 + first
                for lv in range(3):
                    text(g, lv)
            n_pw.leave(6)
            text(8, 1)
            text(8, 2)
            text(9, 2)
            pool.wait_ge(x_done[0], 8)
            pool.wait_ge(z_done[2], 8)
            pool.memset(uv[0:D, 0:HALO, ND * D:], 0.0).then_inc(halo_zero, 1)
            pool.wait_ge(halo_zero, 1)
            pool.memset(uv[D:P, T + HALO:, ND * D:], 0.0).then_inc(halo_zero, 1)
            pool.wait_ge(halo_zero, 2)

            def norm1(n):
                c = chunk_of(n)
                apart(pool, var1, n + 1)
                root(r1[:, :], mm1[:, :, 1], 1.0, EPS, CH, rstd1)
                pool.wait_ge(zs_ready, n + 1)
                v = hall[:, bass.ds(c * CH, CH), :]
                pool.tensor_tensor(v, v, bproj[:, :].unsqueeze(1).to_broadcast([P, CH, D]), ALU.add)\
                    .then_inc(hb_ready, 1)

            def norm2(k):
                apart(pool, var2, k + 1)
                root(r2[:, :], mm2[:, :, 1], 1.0 + EPS, EPS2, CH, rstd2)

            pool.wait_ge(ld_att, ATT_LOADS * 16)
            norm1(0)
            norm1(1)
            norm1(2)
            norm2(0)
            norm1(3)
            norm2(1)
            n_pw.enter(0, 2)
            first = n_pw.start
            with pool.Fori(2, NCH - 2) as k:
                n_pw.base = (k - 2) * 2 + first
                norm1(k + 2)
                norm2(k)
            n_pw.leave(NCH - 4)
            norm2(NCH - 2)
            norm2(NCH - 1)

        @block.scalar
        def _(act):
            for h in range(2):
                act.dma_start(tgc[D * h:D * h + D, :], col("tg")).then_inc(ld_txt, 16)
                act.dma_start(tbc[D * h:D * h + D, :], col("tb")).then_inc(ld_txt, 16)
            act.dma_start(comp[:, :, :], x["comp"].rearrange("(c p) d -> p c d", p=P)).then_inc(ld_txt, 16)
            act.dma_start(opT[:, :], x["opT"]).then_inc(ld_txt, 16)
            act.wait_ge(zeroed, 1)
            act.dma_start(wall[:, 0, :], x["wbin"][D:3 * D, :]).then_inc(ld_txt, 16)
            act.dma_start(wall[0:D, 1, :], x["wbin"][0:D, :]).then_inc(ld_txt, 16)
            act.dma_start(wall[0:D, 2, :], x["wbin"][2 * D:3 * D, :]).then_inc(ld_txt, 16)
            act.dma_start(wall[0:1, 3, :], x["bbin"].rearrange("(a n) -> a n", a=1)).then_inc(ld_txt, 16)
            act.dma_start(tgr[:, :], row("tg", P)).then_inc(ld_txt, 16)
            act.dma_start(tbr[:, :], row("tb", P)).then_inc(ld_txt, 16)
            act.dma_start(wqkvT[:, :, :, :], x["wqkvT"]).then_inc(ld_att, 16)
            act.dma_start(wproj[:, :], x["wproj"]).then_inc(ld_att, 16)
            act.dma_start(bproj[:, :], row("bproj", P)).then_inc(ld_att, 16)
            act.wait_ge(zeroed, 3)
            for j in range(8):
                act.dma_start(wbd[8 * j:8 * j + 8, j, :], x["wemb"]).then_inc(ld_emb, 16)

            act.wait_ge(zct_done, 1)
            act.copy(zcT[:, :, :], PS[0:D, 6, 0:2 * P].rearrange("p (c n) -> p c n", c=2)).then_inc(zct_saved, 1)
            for q in range(4):
                act.wait_ge(o1_done, q + 1)
                act.copy(o1[:, :, 16 * q:16 * q + 16].rearrange("p g b -> p b g"),
                         PS[:, q, :].rearrange("p (b g) -> p b g", b=16)).then_inc(o1_saved, 1)
            for q, i0, n, w in ((0, 0, 2, P), (0, 2, 2, D), (1, 4, 2, D)):
                act.wait_ge(yt_done, q + 1)
                c = (i0 % 4) * P
                act.copy(yt[:, i0:i0 + n, 0:w],
                         PS[0:D, 6 + q, c:c + n * P].rearrange("p (i n) -> p i n", i=n)[:, :, 0:w]).then_inc(yt_saved, 1)
            for i in range(6):
                act.wait_ge(emb_done, i + 1)
                parts = P if i < 2 else D
                act.copy(hall[0:parts, 8 * i:8 * i + 8, :],
                         PS[0:parts, i, :].rearrange("p (j d) -> p j d", d=D)).then_inc(emb_saved, 1)
            for q in range(4):
                act.wait_ge(idT_done, q + 1)
                act.copy(idsT[:, 512 * q:512 * q + 512],
                         PS[0:NID, q % 2, 0:256].bitcast(BF16)).then_inc(idT_saved, 1)

            def spread(v):
                for r in range(NLEAF + NOP):
                    s = r % 3
                    act.wait_ge(bc_done, v * 15 + r + 1)
                    if not (isinstance(v, int) and r < 3):
                        act.wait_ge(bc_used, v * 15 + r - 2)
                    act.copy(bcb[:, s, :], PS[:, s, :]).then_inc(bc_saved, 1)

            spread(0)
            with act.Fori(1, 4) as v:
                spread(v)

            def square(g, lv):
                a, n = ((0, 8), (8, 4), (12, 2))[lv]
                act.wait_ge(x_done[lv], g - lv + 1)
                if not (isinstance(g, int) and g - lv < 1):
                    act.wait_ge(ss_done[lv], g - lv)
                src = PS[:, 4, 0:512] if lv == 0 else (PS[:, 5, 0:256] if lv == 1 else PS[:, 6, 0:128])
                act.activation(sq[:, a:a + n, :], src.rearrange("p (n d) -> p n d", d=D), ACT.Square)\
                    .then_inc(sq_done[lv], 1)

            def save_zt(g, lv):
                act.wait_ge(zt_done[lv], g - lv)
                if lv == 0:
                    act.copy(z1T[:, :, :], PS[:, 0, :].rearrange("p (n q) -> p n q", n=4)).then_inc(zt_saved[0], 1)
                else:
                    act.copy(z2T_[:, :, :], PS[:, 1, 0:256].rearrange("p (n q) -> p n q", n=2)).then_inc(zt_saved[1], 1)

            def text(g, do):
                if "t1" in do:
                    save_zt(g, 0)
                if "t2" in do:
                    save_zt(g, 1)
                for lv in range(3):
                    if f"x{lv}" in do:
                        square(g, lv)

            text(0, TEXT_STEPS[0])
            text(1, TEXT_STEPS[1])
            with act.Fori(2, 8) as g:
                text(g, TEXT_ALL)
            text(8, TEXT_STEPS[8])
            text(9, TEXT_STEPS[9])

            def norm1(n):
                c = chunk_of(n)
                act.wait_ge(ztp_done, n + 1)
                if not (isinstance(n, int) and n == 0):
                    act.wait_ge(uv_done, n * CH)
                act.copy(zT[:, :, :], PS[:, 0, :].rearrange("p (t n) -> p t n", t=CH)).then_inc(zT_ready, 1)
                for t in range(CH):
                    act.wait_ge(uv_done, n * CH + t + 1)
                    act.copy(uv[:, bass.ds(c * CH + HALO + t, 1), :],
                             PS[:, 1 - t % 2, 0:2 * ND * D].unsqueeze(1)).then_inc(uv_saved, 1)

            def softmax(k):
                act.wait_ge(sm_ready, k + 1)
                act.activation(ex[:, :, :], lg[:, :, :], ACT.Exp).then_inc(ex_ready, 1)

            def norm2(k):
                act.wait_ge(z2tp_done, k + 1)
                act.copy(z2T[:, :, :], PS[:, 0, :].rearrange("p (t n) -> p t n", t=CH)).then_inc(z2T_ready, 1)

            def router(k):
                act.wait_ge(dm_ready, k + 1)
                act.activation(th[:, :], dm[:, :], ACT.Tanh, scale=0.5).then_inc(th_ready, 1)

            def experts(k):
                for e in range(NE):
                    act.wait_ge(h_done, k * NE + e + 1)
                    if not (isinstance(k, int) and k == 0 and e < 2):
                        act.wait_ge(y2_done, k * NE + e - 1)
                    act.activation(hT[:, e % 2, :, :], PS[:, 2 + e % 2, :].rearrange("p (t n) -> p t n", t=CH),
                                   ACT.Gelu, bias=b1[:, e:e + 1]).then_inc(h_saved, 1)

            norm1(0)
            v0 = ND * D
            act.wait_ge(uv_saved, CH)
            act.copy(uv[D:P, 0:HALO, v0:], uv[0:D, T:T + HALO, v0:])
            norm1(1)
            act.wait_ge(uv_saved, 2 * CH)
            act.copy(uv[0:D, T + HALO:, v0:], uv[D:P, HALO:2 * HALO, v0:]).then_inc(halo_v, 1)
            norm1(2)
            softmax(0)
            norm2(0)
            act.wait_ge(ffn_ready, 1)

            def turn(k):
                norm1(k + 2)
                router(k - 1)
                experts(k - 1)
                softmax(k)
                norm2(k)

            turn(1)
            with act.Fori(2, NCH - 2) as k:
                turn(k)
            for k in (NCH - 2, NCH - 1):
                router(k - 1)
                experts(k - 1)
                softmax(k)
                norm2(k)
            router(NCH - 1)
            experts(NCH - 1)

        @block.tensor
        def _(pe):
            def mm(out, lhsT, rhs, start, stop):
                return pe.matmul(out, lhsT, rhs, start=start, stop=stop, skip_group_check=True)

            pe.wait_ge(ld_const, 64)
            pe.wait_ge(consts, 1)
            pe.wait_ge(zc_ready, 1)
            for c in range(2):
                i = pe.transpose(PS[0:D, 6, P * c:P * c + P], zc[:, c, :], ident[:, :])
            i.then_inc(zct_done, 1)
            pe.wait_ge(wc_ready, 1)
            pe.wait_ge(zct_saved, 1)
            pe.wait_ge(ld_txt, TXT_LOADS * 16)
            for c in range(2):
                mm(PS[:, 5, P * c:P * c + D], zcT[:, c, :], wg[0:D, 0, :], True, True)
                mm(PS[:, 5, P * c + D:P * c + P], zcT[:, c, :], wg[0:D, 2, :], True, True)
            for h in range(2):
                o = PS[D * h:D * h + D, 5, 4 * D:5 * D]
                mm(o, opT[:, :], wall[0:D, 1, :], True, False)
                mm(o, tbc[:, :].to_broadcast([P, D]), wall[:, 0, :], False, False)
                i = mm(o, ones[:, 0:D], wall[0:1, 3, :], False, True)
            i.then_inc(tab_done, 1)
            pe.wait_ge(ld_att, ATT_LOADS * 16)
            for i in range(ND):
                for h in range(2):
                    o = PS[D * h:D * h + D, 7, :]
                    mm(o[:, D * i:D * i + D], wqkvT[:, i, 0, :], wqkvT[:, i, 1, :], True, True)
                    last = mm(o[:, D * (ND + i):D * (ND + i) + D], wqkvT[:, i, 2, :], wproj[:, :], True, True)
            last.then_inc(mv_done, 1)

            for b in range(B):
                if b % 16 == 0:
                    pe.wait_ge(ld_img[b // 16], 16)
                i = mm(PS[:, b // 16, G8 * (b % 16):G8 * (b % 16) + G8], img[:, b, :], gt[:, :], True, True)
                if b % 16 == 15:
                    i.then_inc(o1_done, 1)
            pe.wait_ge(o1_saved, 4)
            pe.wait_ge(tab_ready, 1)
            for g in range(NG):
                for r in range(8):
                    half, i8_ = (0, r) if r < 6 else (1, r - 6)
                    c = (i8_ % 4) * P + g * G8
                    i = mm(PS[D * half:D * half + D, 4 + i8_ // 4, c:c + G8], o1[:, 8 * g + r, :], gt[:, :], True, True)
            i.then_inc(y_done, 1)
            pe.wait_ge(ya_ready, 1)
            pe.wait_ge(mv_ready, 1)
            for i in range(6):
                n = P if i < 2 else D
                q = i // 4
                c = (i % 4) * P
                last = pe.transpose(PS[0:D, 6 + q, c:c + n],
                                    ya[0:n, 8 * i:8 * i + 8, :].rearrange("p j m -> p (j m)"), ident[0:n, 0:n])
                if i in (3, 5):
                    last.then_inc(yt_done, 1)
            pe.wait_ge(ld_emb, 128)
            for i in range(6):
                if i % 4 == 0:
                    pe.wait_ge(yt_saved, (2, 3)[i // 4])
                n = P if i < 2 else D
                mm(PS[0:n, i, :], yt[:, i, 0:n], wbd[:, :, :].rearrange("p j d -> p (j d)"), True, True)\
                    .then_inc(emb_done, 1)

            pe.wait_ge(ld_ffn, FFN_LOADS * 16)
            for e in range(NE):
                mm(PS[:, 7, e:e + 1], w1[0:D, HID * e:HID * e + HID], fbc[0:D, :], True, True)
            mm(PS[:, 7, NE:2 * NE], fbc[0:D, :].to_broadcast([D, P]), wr[0:D, :], True, False)
            mm(PS[:, 7, NE:2 * NE], ones[:, :], brow[:, :], False, True).then_inc(bias_done, 1)

            pe.wait_ge(idb_ready, 1)
            pe.wait_ge(emb_saved, 6)
            for q in range(4):
                if q >= 2:
                    pe.wait_ge(idT_saved, q - 1)
                for s in range(4):
                    i = pe.transpose(PS[0:NID, q % 2, 64 * s:64 * s + 64].bitcast(BF16), idb[:, 4 * q + s, :], identb[:, :])
                i.then_inc(idT_done, 1)
            pe.wait_ge(idT_saved, 4)

            def spread(v):
                for r in range(NLEAF + NOP):
                    if not (isinstance(v, int) and r < 3):
                        apart(pe, bc_saved, v * 15 + r - 2, True)
                    mm(PS[:, r % 3, :], identb[0:NID, r:r + 1].to_broadcast([NID, P]),
                       idsT[:, bass.ds(v * VB, VB)], True, True).then_inc(bc_done, 1)

            spread(0)
            with pe.Fori(1, 4) as v:
                spread(v)

            def text(g, do):
                if "t1" in do:
                    pe.wait_ge(z_done[0], g)
                    for n in range(4):
                        i = pe.transpose(PS[:, 0, P * n:P * n + P],
                                         z1[:, 2 * n:2 * n + 2, :].rearrange("p n d -> p (n d)"), ident[:, :])
                    i.then_inc(zt_done[0], 1)
                if "t2" in do:
                    pe.wait_ge(z_done[1], g - 1)
                    for n in range(2):
                        i = pe.transpose(PS[:, 1, P * n:P * n + P],
                                         z2[:, 2 * n:2 * n + 2, :].rearrange("p n d -> p (n d)"), ident[:, :])
                    i.then_inc(zt_done[1], 1)
                if "x0" in do:
                    for s in range(2):
                        at_ = lambda r: r[:, bass.ds((g * 2 + s) * P, P)]
                        for k in range(4):
                            o = PS[:, 4, D * (4 * s + k):D * (4 * s + k) + D]
                            first = True
                            for side in range(2):
                                for c in range(2):
                                    for part in range(3):
                                        mm(o, at_(onehot[:, 2 * (2 * k + side) + c, :]),
                                           tab[:, part, P * c + D * side:P * c + D * side + D], first, False)
                                        first = False
                            for part in range(2):
                                i = mm(o, at_(onehot_op[:, k, :]), opab[:, part, :], False, part == 1)
                    i.then_inc(x_done[0], 1)
                if "x1" in do:
                    pe.wait_ge(zt_saved[0], g)
                    for s in range(2):
                        for k in range(2):
                            n = 2 * s + k
                            o = PS[:, 5, D * n:D * n + D]
                            mm(o, z1T[:, n, :], wg[:, 0, :], True, False)
                            for part in range(2):
                                i = mm(o, onehot_op[:, 4 + k, bass.ds((g * 2 - 2 + s) * P, P)],
                                       opab[:, part, :], False, part == 1)
                    i.then_inc(x_done[1], 1)
                if "x2" in do:
                    pe.wait_ge(zt_saved[1], g - 1)
                    if not (isinstance(g, int) and g == 2):
                        pe.wait_ge(z_done[2], g - 2)
                    for s in range(2):
                        o = PS[:, 6, D * s:D * s + D]
                        mm(o, z2T_[:, s, :], wg[:, 0, :], True, False)
                        for part in range(2):
                            i = mm(o, onehot_op[:, 6, bass.ds((g * 2 - 4 + s) * P, P)], opab[:, part, :], False, part == 1)
                    i.then_inc(x_done[2], 1)

            pe.wait_ge(bc_used, 60)
            text(0, TEXT_STEPS[0])
            text(1, TEXT_STEPS[1])
            with pe.Fori(2, 8) as g:
                text(g, TEXT_ALL)
            text(8, TEXT_STEPS[8])
            text(9, TEXT_STEPS[9])

            def norm1(n):
                pe.wait_ge(zs_ready, n + 1)
                if not (isinstance(n, int) and n == 0):
                    pe.wait_ge(uv_saved, n * CH)
                if not (isinstance(n, int) and n < 3):
                    pe.wait_ge(z2T_ready, n - 2)
                for t in range(CH):
                    i = pe.transpose(PS[:, 0, P * t:P * t + P], zs[:, t, :, :].rearrange("p a d -> p (a d)"), ident[:, :])
                i.then_inc(ztp_done, 1)
                pe.wait_ge(zT_ready, n + 1)
                for t in range(CH):
                    if t >= 2:
                        pe.wait_ge(uv_saved, n * CH + t - 1)
                    o = PS[:, 1 - t % 2, 0:2 * ND * D]
                    if t == 0 and not (isinstance(n, int) and n < 3):
                        pe.wait_ge(lg_used, n - 2)
                    mm(o, zT[:, t, :], mvh[:, :], True, False)
                    mm(o, zT[:, t, :], mvl[:, :], False, True).then_inc(uv_done, 1)

            def norm2(k, n_uv):
                pe.wait_ge(z2s_ready, k + 1)
                pe.wait_ge(uv_saved, n_uv)
                for t in range(CH):
                    i = pe.transpose(PS[:, 0, P * t:P * t + P], z2s[:, t, :, :].rearrange("p a d -> p (a d)"), ident[:, :])
                i.then_inc(z2tp_done, 1)
                pe.wait_ge(z2T_ready, k + 1)
                if not (isinstance(k, int) and k == 0):
                    pe.wait_ge(lg_used, k)
                for t in range(CH):
                    o = PS[:, 1, NE * t:NE * t + NE]
                    mm(o, z2T[:, t, :], wrh[:, :], True, False)
                    i = mm(o, z2T[:, t, :], wrl[:, :], False, True)
                i.then_inc(lg_done, 1)

            def hidden(k, e):
                o = PS[:, 2 + e % 2, :]
                z = z2T[:, :, :].rearrange("p t n -> p (t n)")
                if not (isinstance(k, int) and k == 0 and e < 2):
                    pe.wait_ge(h_saved, k * NE + e - 1)
                mm(o, w1h[:, HID * e:HID * e + HID], z, True, False)
                mm(o, w1l[:, HID * e:HID * e + HID], z, False, True).then_inc(h_done, 1)

            def experts(k):
                hidden(k, 0)
                for e in range(NE):
                    if e + 1 < NE:
                        hidden(k, e + 1)
                    if e == 0:
                        for t in range(CH):
                            if not (isinstance(k, int) and k == 0):
                                pe.wait_ge(y2_used, (k - 1) * CH + t + 1)
                            mm(PS[:, 4 + t, :], onesb[:, :], b2p[:, :], True, False)
                    pe.wait_ge(h_saved, k * NE + e + 1)
                    for t in range(CH):
                        i = mm(PS[:, 4 + t, D * e:D * e + D], hT[:, e % 2, t, :], w2[:, e, :], False, e == NE - 1)
                    i.then_inc(y2_done, 1)

            pe.wait_ge(mv_ready, 1)
            norm1(0)
            norm1(1)
            norm1(2)
            pe.wait_ge(ffn_ready, 1)
            norm2(0, 3 * CH)

            def turn(k):
                norm1(k + 2)
                experts(k - 1)
                norm2(k, (k + 3) * CH)

            turn(1)
            with pe.Fori(2, NCH - 2) as k:
                turn(k)
            experts(NCH - 3)
            norm2(NCH - 2, NCH * CH)
            experts(NCH - 2)
            norm2(NCH - 1, NCH * CH)
            experts(NCH - 1)

        @block.vector
        def _(dve):
            own = Count(vec)

            def after(t, bare=False, addressed=False):
                (apart(dve, vec, t, addressed) if bare else dve.wait_ge(vec, t))

            dve.memset(wall[:, :, :], 0.0).then_inc(zeroed, 1)
            dve.memset(b2x[:, :], 0.0).then_inc(zeroed, 1)
            dve.memset(wbd[:, :, :], 0.0).then_inc(zeroed, 1)
            dve.memset(ones[:, :], 1.0)
            dve.memset(onesb[:, :], 1.0)
            own.add(dve.memset(opab[D:P, 1, :], 0.0))
            own.add(dve.memset(b2p[:, :], 0.0))
            own.add(dve.memset(ya[:, :, 7:8], 1.0))
            own.add(dve.memset(zall[0:D, 0:HALO, :], 0.0))
            own.add(dve.memset(zall[D:P, T + HALO:, :], 0.0))
            dve.wait_ge(ld_const, 64)
            dve.tensor_copy(identb[:, :], ident[:, :]).then_inc(consts, 1)

            dve.wait_ge(ld_txt, TXT_LOADS * 16)
            for c in range(2):
                t = own.add(dve.bn_stats(stc[:, c, :], comp[:, c, :]))
            after(t)
            for c in range(2):
                i = dve.bn_aggr(mvc[:, c, :], stc[:, c, :])
            i.then_inc(vc_ready, 1)
            t = own.add(dve.tensor_reduce(wsum[:, :], wall[:, :, :], AX.X, ALU.add))
            after(t)
            t = own.add(dve.tensor_scalar(wsum[:, :], wsum[:, :], 1.0 / D, None, ALU.mult))
            after(t)
            t = own.add(dve.tensor_tensor(wall[:, :, :], wall[:, :, :],
                                          wsum[:, :].unsqueeze(2).to_broadcast([P, 4, D]), ALU.subtract))
            after(t)
            for s in (0, 2):
                i = dve.tensor_scalar(wg[:, s, :], wall[:, s, :], tgc[:, 0:1], None, ALU.mult)
            i.then_inc(wc_ready, 1)
            dve.wait_ge(rc_ready, 1)
            for c in range(2):
                i = dve.tensor_scalar(zc[:, c, :], comp[:, c, :], mvc[:, c, 0:1], rc[:, c:c + 1],
                                      ALU.subtract, ALU.mult)
            i.then_inc(zc_ready, 1)
            dve.wait_ge(tab_done, 1)
            src = PS[:, 5, 0:5 * D]
            t = own.add(dve.tensor_copy(tab[:, 0, :], src))
            after(t)
            t = own.add(dve.tensor_tensor(tabr[:, :], src, tab[:, 0, :], ALU.subtract))
            after(t)
            t = own.add(dve.tensor_copy(tab[:, 1, :], tabr[:, :]))
            after(t)
            t = own.add(dve.tensor_tensor(tabr[:, :], tabr[:, :], tab[:, 1, :], ALU.subtract))
            after(t)
            t = own.add(dve.tensor_copy(tab[:, 2, :], tabr[:, :]))
            after(t)
            dve.tensor_copy(opab[0:D, 0, :], tab[0:D, 0, 4 * D:])
            dve.tensor_copy(opab[D:P, 0, :], tab[D:P, 1, 4 * D:])
            dve.tensor_copy(opab[0:D, 1, :], tab[0:D, 2, 4 * D:]).then_inc(tab_ready, 1)
            dve.wait_ge(mv_done, 1)
            nu = ND * D
            own.add(dve.tensor_scalar(mv32[:, 0:nu], PS[:, 7, 0:nu], float(D) ** -0.5, None, ALU.mult))
            t = own.add(dve.tensor_scalar(mv32[:, nu:], PS[:, 7, nu:2 * nu], 1.0 / ND, None, ALU.mult))
            after(t)
            t = own.add(dve.tensor_copy(mvh[:, :], mv32[:, :]))
            after(t)
            dve.tensor_tensor(mvl[:, :], mv32[:, :], mvh[:, :].bitcast(F32), ALU.subtract).then_inc(mv_ready, 1)

            t = own.add(dve.tensor_copy(mask[:, :], tok[:, :]))
            after(t)
            dve.tensor_scalar(mask[:, :], mask[:, :], 1.0, None, ALU.is_gt).then_inc(mask_ready, 1)

            dve.wait_ge(y_done, 1)
            y = PS[:, 4:6, :].rearrange("p a n -> p (a n)")
            for n, half in ((6, 0), (2, 1)):
                p0 = D * half
                for g2 in range(2):
                    dst = bass.AP(tensor=ya[:, :, :].tensor, offset=ya[p0:p0 + D, 0:1, 2 * g2:2 * g2 + 1].offset,
                                  ap=[[T * 8, D], [64, n], [1, 2], [8, 8]])
                    s = y[p0:p0 + D, 0:n * P].rearrange("p (i g h j) -> p i g h j", i=n, g=NG, h=NG)
                    dve.tensor_copy(dst, s[:, :, 0:2, g2, :])
                for m, (g, g2) in ((4, (3, 2)), (5, (2, 3)), (6, (3, 3))):
                    dst = bass.AP(tensor=ya[:, :, :].tensor, offset=ya[p0:p0 + D, 0:1, m:m + 1].offset,
                                  ap=[[T * 8, D], [64, n], [8, 8]])
                    s = y[p0:p0 + D, 0:n * P].rearrange("p (i g h j) -> p i g h j", i=n, g=NG, h=NG)
                    i = dve.tensor_copy(dst, s[:, :, g, g2, :])
            i.then_inc(ya_ready, 1)

            dve.wait_ge(ld_ffn, FFN_LOADS * 16)
            dve.wait_ge(ld_b2, 48)
            own.add(dve.tensor_scalar(w1h[:, :], w1[:, :], fgc[:, 0:1], None, ALU.mult))
            own.add(dve.tensor_scalar(wrh[:, :], wr[:, :], fgc[:, 0:1], None, ALU.mult))
            t = own.add(dve.tensor_copy(b2b[:, :], b2x[:, :]))
            after(t)
            dve.scalar_tensor_tensor(w1l[:, :], w1[:, :], fgc[:, 0:1], w1h[:, :].bitcast(F32), ALU.mult, ALU.subtract)
            dve.scalar_tensor_tensor(wrl[:, :], wr[:, :], fgc[:, 0:1], wrh[:, :].bitcast(F32), ALU.mult, ALU.subtract)
            own.add(dve.tensor_copy(b2p[0:1, :], b2b[0:1, :]))
            t = own.add(dve.tensor_tensor(b2x[:, :], b2x[:, :], b2b[:, :], ALU.subtract))
            after(t)
            t = own.add(dve.tensor_copy(b2b[:, :], b2x[:, :]))
            after(t)
            own.add(dve.tensor_copy(b2p[32:33, :], b2b[32:33, :]))
            t = own.add(dve.tensor_tensor(b2x[:, :], b2x[:, :], b2b[:, :], ALU.subtract))
            after(t)
            dve.tensor_copy(b2p[64:65, :], b2x[64:65, :])
            dve.wait_ge(bias_done, 1)
            own.add(dve.tensor_copy(br[:, :], PS[:, 7, NE:2 * NE]))
            dve.tensor_tensor(b1[:, :], b1[:, :], PS[:, 7, 0:NE], ALU.add).then_inc(ffn_ready, 1)

            dve.wait_ge(gathered, 16 * SP)
            dve.tensor_copy(idb[:, :, :], idg[:, :, :]).then_inc(idb_ready, 1)

            def spread(v):
                for r in range(NLEAF + NOP):
                    s = r % 3
                    dve.wait_ge(bc_saved, v * 15 + r + 1)
                    if r < NLEAF:
                        for c in range(2):
                            i = dve.tensor_scalar(onehot[:, 2 * r + c, bass.ds(v * VB, VB)], bcb[:, s, :],
                                                  iota3[:, c:c + 1], None, ALU.is_equal)
                    else:
                        i = dve.tensor_scalar(onehot_op[:, r - NLEAF, bass.ds(v * VB, VB)], bcb[:, s, :],
                                              iota3[:, 2:3], None, ALU.is_equal)
                    i.then_inc(bc_used, 1)

            dve.wait_ge(o1_done, 4)
            with dve.Fori(0, 4) as v:
                spread(v)

            dve.wait_ge(mb_ready, 1)
            LV = ((0, 8, 4), (8, 4, 5), (12, 2, 6))

            def sums(g, lv):
                a, n, _ = LV[lv]
                dve.wait_ge(sq_done[lv], g - lv + 1)
                dve.tensor_reduce(ss[:, a:a + n], sq[:, a:a + n, :], AX.X, ALU.add).then_inc(ss_done[lv], 1)

            def scaled(g, lv):
                a, n, bank = LV[lv]
                dve.wait_ge(rt_done[lv], g - lv + 1)
                src = PS[:, bank, 0:n * D].rearrange("p (n d) -> p n d", d=D)
                if lv < 2:
                    z = z1 if lv == 0 else z2
                    dve.tensor_tensor(z[:, :, :], src, rt[:, a:a + n].unsqueeze(2).to_broadcast([P, n, D]), ALU.mult)\
                        .then_inc(z_done[lv], 1)
                    return
                pair = bass.ds(g * 2 - 4, 2)
                t = own.add(dve.tensor_tensor(rt[:, a:a + n], rt[:, a:a + n], mask[:, pair], ALU.mult))
                after(t)
                t = own.add(dve.tensor_tensor(fin[:, :, :], src, rt[:, a:a + n].unsqueeze(2).to_broadcast([P, n, D]), ALU.mult))
                after(t)
                t = own.add(dve.tensor_tensor(fin[:, :, :], fin[:, :, :], tgr[:, :].unsqueeze(1).to_broadcast([P, n, D]), ALU.mult))
                after(t)
                dst = hall[D:P, :, :].rearrange("p (t s) d -> p t s d", s=2)[:, bass.ds(g * 2 - 4 + TXT_T // 2, 2), :, :]
                for s in range(2):
                    i = dve.tensor_tensor(dst[:, :, s, :], fin[D * s:D * s + D, :, :], mbeta[D * s:D * s + D, pair, :], ALU.add)
                i.then_inc(z_done[2], 1)

            def text(g, do):
                for lv in range(3):
                    if f"x{lv}" in do:
                        sums(g, lv)
                for lv in range(3):
                    if f"x{lv}" in do:
                        scaled(g, lv)

            text(0, TEXT_STEPS[0])
            text(1, TEXT_STEPS[1])
            own.enter(0, 3)
            first = own.start
            with dve.Fori(2, 8) as g:
                own.base = (g - 2) * 3 + first
                text(g, TEXT_ALL)
            own.leave(6)
            text(8, TEXT_STEPS[8])
            text(9, TEXT_STEPS[9])

            def tiles(c):
                return bass.ds(c * CH, CH)

            def stats1(n):
                c = chunk_of(n)
                for t_ in range(CH):
                    t = own.add(dve.bn_stats(st1[:, t_, :], hall[:, bass.ds(c * CH + t_, 1), :].squeeze(1)))
                after(t, True)
                for t_ in range(CH):
                    i = dve.bn_aggr(mm1[:, t_, :], st1[:, t_, :])
                i.then_inc(var1, 1)

            def z1_(n):
                c = chunk_of(n)
                dve.wait_ge(rstd1, n + 1)
                if not (isinstance(n, int) and n == 0):
                    dve.wait_ge(ztp_done, n)
                for t_ in range(CH):
                    t = own.add(dve.tensor_scalar(zall[:, bass.ds(c * CH + t_ + HALO, 1), :].squeeze(1),
                                                  hall[:, bass.ds(c * CH + t_, 1), :].squeeze(1),
                                                  mm1[:, t_, 0:1], r1[:, t_:t_ + 1], ALU.subtract, ALU.mult))
                after(t, True, True)
                z = zall[:, bass.ds(c * CH + HALO, CH), :]
                t = own.add(dve.tensor_copy(zs[:, :, 0, :].bitcast(F32R), z))
                after(t)
                dve.tensor_tensor(zs[:, :, 1, :], z, zs[:, :, 0, :], ALU.subtract).then_inc(zs_ready, 1)

            def scores(k, n_uv):
                dve.wait_ge(uv_saved, n_uv)
                for i in range(ND):
                    d = DIL[i]
                    pr = ap_of(prod[:, CH * KW * D * i:CH * KW * D * i + 1], [[KW * D, CH], [D, KW], [1, D]])
                    u = ap_of(uv[:, bass.ds(k * CH + HALO, 1), D * i:D * i + 1], [[2 * ND * D, CH], [0, KW], [1, D]])
                    z = ap_of(zall[:, bass.ds(k * CH + HALO - d, 1), 0:1], [[D, CH], [d * D, KW], [1, D]])
                    t = own.add(dve.tensor_tensor(pr, u, z, ALU.mult))
                    after(t)
                    t = own.add(dve.tensor_reduce(lg[:, :, KW * i:KW * i + KW], pr, AX.X, ALU.add))
                after(t)
                l3 = lg[:, :, :].rearrange("p t (i k) -> p (t i) k", k=KW)
                t = own.add(dve.tensor_reduce(mx[:, :], l3, AX.X, ALU.max))
                after(t)
                dve.tensor_tensor(l3, l3, mx[:, :].unsqueeze(2).to_broadcast([P, CH * ND, KW]), ALU.subtract)\
                    .then_inc(sm_ready, 1)

            def attend(k, n_uv):
                dve.wait_ge(ex_ready, k + 1)
                e3 = ex[:, :, :].rearrange("p t (i k) -> p (t i) k", k=KW)
                a3 = at[:, :, :].rearrange("p t (i k) -> p (t i) k", k=KW)
                t = own.add(dve.tensor_reduce(sm[:, :], e3, AX.X, ALU.add))
                after(t)
                t = own.add(dve.reciprocal(rs[:, :], sm[:, :]))
                after(t)
                t = own.add(dve.tensor_tensor(a3, e3, rs[:, :].unsqueeze(2).to_broadcast([P, CH * ND, KW]), ALU.mult))
                after(t)
                dve.wait_ge(uv_saved, n_uv)
                J = ND * KW
                for i in range(ND):
                    d = DIL[i]
                    pr = ap_of(prod[:, D * KW * i:D * KW * i + 1], [[J * D, CH], [D, KW], [1, D]])
                    a = ap_of(at[:, 0:1, KW * i:KW * i + 1], [[J, CH], [1, KW], [0, D]])
                    v = ap_of(uv[:, bass.ds(k * CH + HALO - d, 1), D * (ND + i):D * (ND + i) + 1],
                              [[2 * ND * D, CH], [d * 2 * ND * D, KW], [1, D]])
                    t = own.add(dve.tensor_tensor(pr, a, v, ALU.mult))
                after(t)
                t = own.add(dve.tensor_reduce(av[:, :, :], ap_of(prod[:, 0:1], [[J * D, CH], [1, D], [D, J]]), AX.X, ALU.add))
                after(t)

            def stats2(k, n_hb):
                dve.wait_ge(hb_ready, n_hb)
                h = hall[:, tiles(k), :]
                t = own.add(dve.tensor_tensor(h, h, av[:, :, :], ALU.add))
                after(t, True, True)
                for t_ in range(CH):
                    t = own.add(dve.bn_stats(st2[:, t_, :], hall[:, bass.ds(k * CH + t_, 1), :].squeeze(1)))
                after(t, True)
                for t_ in range(CH):
                    i = dve.bn_aggr(mm2[:, t_, :], st2[:, t_, :])
                i.then_inc(var2, 1)

            def z2_(k):
                dve.wait_ge(rstd2, k + 1)
                if not (isinstance(k, int) and k == 0):
                    dve.wait_ge(z2tp_done, k)
                for t_ in range(CH):
                    t = own.add(dve.tensor_scalar(z32[:, t_, :], hall[:, bass.ds(k * CH + t_, 1), :].squeeze(1),
                                                  mm2[:, t_, 0:1], r2[:, t_:t_ + 1], ALU.subtract, ALU.mult))
                after(t)
                t = own.add(dve.tensor_copy(z2s[:, :, 0, :].bitcast(F32R), z32[:, :, :]))
                after(t)
                dve.tensor_tensor(z2s[:, :, 1, :], z32[:, :, :], z2s[:, :, 0, :], ALU.subtract).then_inc(z2s_ready, 1)

            def top2(k):
                dve.wait_ge(lg_done, k + 1)
                t = own.base + own.n
                dve.tensor_tensor(rl[:, :, :], PS[:, 1, 0:CH * NE].rearrange("p (t e) -> p t e", e=NE),
                                  br[:, :].unsqueeze(1).to_broadcast([P, CH, NE]), ALU.add).then_inc(lg_used, 1)
                apart(dve, lg_used, k + 1)
                for t_ in range(CH):
                    t = own.add(dve.max(v8[:, t_, :], rl[:, t_, :]))
                after(t)
                dve.tensor_tensor(dm[:, :], v8[:, :, 1], v8[:, :, 0], ALU.subtract).then_inc(dm_ready, 1)
                for t_ in range(CH):
                    t = own.add(dve.max_index(i8[:, t_, :], v8[:, t_, :], rl[:, t_, :]))
                after(t)
                t = own.add(dve.tensor_copy(i8f[:, :, :], i8[:, :, 0:2]))
                after(t)
                io = iota8[:, :].unsqueeze(1).to_broadcast([P, CH, NE])
                own.add(dve.tensor_tensor(se1[:, :, :], io, i8f[:, :, 0:1].to_broadcast([P, CH, NE]), ALU.is_equal))
                t = own.add(dve.tensor_tensor(se2[:, :, :], io, i8f[:, :, 1:2].to_broadcast([P, CH, NE]), ALU.is_equal))

            def weights(k):
                dve.wait_ge(th_ready, k + 1)
                own.add(dve.tensor_scalar(tw[:, :, 0], th[:, :], -0.5, 0.5, ALU.mult, ALU.add))
                t = own.add(dve.tensor_scalar(tw[:, :, 1], th[:, :], 0.5, 0.5, ALU.mult, ALU.add))
                after(t)
                own.add(dve.tensor_tensor(se1[:, :, :], se1[:, :, :], tw[:, :, 0:1].to_broadcast([P, CH, NE]), ALU.mult))
                t = own.add(dve.tensor_tensor(se2[:, :, :], se2[:, :, :], tw[:, :, 1:2].to_broadcast([P, CH, NE]), ALU.mult))
                after(t)
                t = own.add(dve.tensor_tensor(wf[:, :, :], se1[:, :, :], se2[:, :, :], ALU.add))
                after(t)

            def combine(k, some):
                dve.wait_ge(y2_done, k * NE + NE)
                ts = []
                for t_ in some:
                    i = dve.tensor_tensor(yw[:, t_ % 2, :, :], PS[:, 4 + t_, :].rearrange("p (e d) -> p e d", d=D),
                                          wf[:, t_, :].unsqueeze(2).to_broadcast([P, NE, D]), ALU.mult)
                    i.then_inc(y2_used, 1)
                    dve.wait_ge(y2_used, k * CH + t_ + 1)
                    t = own.add(dve.tensor_reduce(yo[:, t_, :], yw[:, t_ % 2, :, :].rearrange("p e d -> p d e"), AX.X, ALU.add))
                if some[-1] == CH - 1:
                    after(t)
                    h = hall[:, tiles(k), :]
                    dve.tensor_tensor(h, h, yo[:, :, :], ALU.add).then_inc(out_ready, 1)

            dve.wait_ge(emb_saved, 6)
            dve.wait_ge(z_done[2], 8)
            stats1(0)
            z1_(0)
            dve.wait_ge(zs_ready, 1)
            t = own.add(dve.tensor_copy(zall[D:P, 0:HALO, :], zall[0:D, T:T + HALO, :]))
            stats1(1)
            z1_(1)
            t = own.add(dve.tensor_copy(zall[0:D, T + HALO:, :], zall[D:P, HALO:2 * HALO, :]))
            stats1(2)
            z1_(2)
            dve.wait_ge(zs_ready, 3)
            dve.wait_ge(halo_v, 1)
            dve.wait_ge(halo_zero, 2)
            scores(0, 2 * CH)
            attend(0, 3 * CH)
            stats2(0, 2)
            z2_(0)

            def turn(k):
                stats1(k + 2)
                top2(k - 1)
                z1_(k + 2)
                dve.wait_ge(zs_ready, k + 3)
                scores(k, (k + 2) * CH)
                weights(k - 1)
                combine(k - 1, (0, 1))
                attend(k, (k + 3) * CH)
                stats2(k, k + 2)
                combine(k - 1, (2, 3))
                z2_(k)

            turn(1)
            per = 53
            own.enter(0, per)
            first = own.start
            with dve.Fori(2, NCH - 2) as k:
                own.base = (k - 2) * per + first
                turn(k)
            own.leave(NCH - 4)
            for k in (NCH - 2, NCH - 1):
                top2(k - 1)
                scores(k, NCH * CH)
                weights(k - 1)
                combine(k - 1, (0, 1))
                attend(k, NCH * CH)
                stats2(k, NCH)
                combine(k - 1, (2, 3))
                z2_(k)
            top2(NCH - 1)
            weights(NCH - 1)
            combine(NCH - 1, (0, 1, 2, 3))


TXT_LOADS = 12
ATT_LOADS = 3
FFN_LOADS = 11
TEXT_ALL = ("t1", "t2", "x0", "x1", "x2")
TEXT_STEPS = {0: ("x0",), 1: ("t1", "x0", "x1"), 8: ("t1", "t2", "x1", "x2"), 9: ("t2", "x2")}


def operators():
    s = 0.7071067811865476

    def haar(n, sign):
        m = np.zeros((n // 2, n))
        m[np.arange(n // 2), 2 * np.arange(n // 2)] = s
        m[np.arange(n // 2), 2 * np.arange(n // 2) + 1] = sign * s
        return m

    def resize(n):
        f = n / 8
        at = (np.arange(8) + 0.5) * f - 0.5
        w = np.maximum(0, 1 - np.abs(at[:, None] - np.arange(n)[None, :]) / f)
        return w / w.sum(1, keepdims=True)

    lo, hi = haar(IMG, 1), haar(IMG, -1)
    rows = [resize(32) @ haar(64, 1) @ lo, resize(32) @ haar(64, -1) @ lo, resize(64) @ lo, resize(64) @ hi]
    return np.ascontiguousarray(np.concatenate(rows, 0).T.astype(np.float32))


def kernel(x, x_txt, L0_tok_W, L0_tok_b, L0_txt_leaf_ids, L0_txt_op_ids, L0_txt_comp_emb, L0_txt_op_emb,
           L0_txt_W_bin, L0_txt_b_bin, L0_txt_gamma, L0_txt_beta, L0_attn_Wqkv, L0_attn_Wproj, L0_attn_bproj,
           L0_ffn_gamma, L0_ffn_beta, L0_ffn_Wr, L0_ffn_br, L0_ffn_W1, L0_ffn_b1, L0_ffn_W2, L0_ffn_b2):
    import concourse.bacc as bacc
    from concourse.bass_utils import run_bass_kernel_spmd

    A = np.asarray
    cat = np.concatenate
    leaf, op = A(L0_txt_leaf_ids), A(L0_txt_op_ids)
    arrays = {
        "img": A(x)[:, 0].transpose(1, 0, 2),
        "tok": A(x_txt).reshape(B, SP, 2).transpose(2, 0, 1).reshape(P, SP),
        "ids": cat([leaf, op, np.zeros((leaf.shape[0], NID - NLEAF - NOP), leaf.dtype)], 1),
        "wemb": cat([A(L0_tok_W), A(L0_tok_b)[None, :]], 0),
        "comp": A(L0_txt_comp_emb), "opT": A(L0_txt_op_emb).T,
        "wbin": A(L0_txt_W_bin), "bbin": A(L0_txt_b_bin), "tg": A(L0_txt_gamma), "tb": A(L0_txt_beta),
        "wqkvT": A(L0_attn_Wqkv).reshape(ND, D, 3, D).transpose(3, 0, 2, 1),
        "wproj": A(L0_attn_Wproj), "bproj": A(L0_attn_bproj),
        "fg": A(L0_ffn_gamma), "fb": A(L0_ffn_beta), "wr": A(L0_ffn_Wr), "br": A(L0_ffn_br),
        "w1": A(L0_ffn_W1).transpose(1, 0, 2).reshape(D, NE * HID), "b1": A(L0_ffn_b1).T,
        "w2": A(L0_ffn_W2).transpose(1, 0, 2), "b2": A(L0_ffn_b2).reshape(-1),
        "ident": np.eye(P, dtype=np.float32), "gt": operators(),
        "iota3": np.stack([np.arange(P), np.arange(P) + P, np.arange(P) % D], 1).astype(np.float32),
        "iota8": np.tile(np.arange(NE, dtype=np.float32), (P, 1)),
    }
    arrays = {n: np.ascontiguousarray(a) for n, a in arrays.items()}
    nc = bacc.Bacc("TRN2", target_bir_lowering=False, num_devices=1)
    tensors = {n: nc.dram_tensor(f"in_{n}", a.shape, mybir.dt.from_np(a.dtype), kind="ExternalInput").ap()
               for n, a in arrays.items()}
    tensors["out"] = nc.dram_tensor("out_0", (B, NTOK, D), F32, kind="ExternalOutput").ap()
    build(nc, tensors)
    r = run_bass_kernel_spmd(nc, [{f"in_{n}": a for n, a in arrays.items()}], core_ids=[0])
    return r.results[0]["out_0"]
```

```python
from contextlib import ExitStack

import numpy as np
import concourse.bass as bass
from concourse import mybir

F32 = mybir.dt.float32
F32R = mybir.dt.float32r
BF16 = mybir.dt.bfloat16
I32 = mybir.dt.int32
U32 = mybir.dt.uint32
ALU = mybir.AluOpType
ACT = mybir.ActivationFunctionType
AX = mybir.AxisListType

P = 128
B = 64
D = 64
NTOK = 96
T = NTOK // 2
TXT_T = 16
CH = 4
NCH = T // CH
HALO = 3
DIL = (1, 2, 3)
ND = 3
KW = 3
EPS = 1e-5
EPS2 = EPS * EPS
IMG = 128
NG = 4
G8 = 8 * NG
NLEAF = 8
NOP = 7
NID = 16
SP = 16
TXT = 2048
VB = 512
NE = 8
HID = 128
NHT = 4


def ap_of(view, dims):
    return bass.AP(tensor=view.tensor, offset=view.offset, ap=[list(view.ap[0]), *dims])


class Count:

    def __init__(self, sem):
        self.sem, self.base, self.n = sem, 0, 0

    def add(self, ins):
        ins.then_inc(self.sem, 1)
        self.n += 1
        return self.base + self.n

    def value(self):
        return self.base + self.n

    def enter(self, turns, per):
        self.outer, self.per, self.start = (self.base, self.n), per, self.base + self.n
        self.base, self.n = turns * per + self.start, 0

    def leave(self, turns):
        assert self.n == self.per, (self.n, self.per)
        self.base, self.n = self.start + turns * self.per, 0


def build(nc, x):
    ctx = ExitStack()
    with ctx:
        def sb(name, shape, dt=F32):
            return ctx.enter_context(nc.sbuf_tensor(name, shape, dt))

        def sem(name):
            return ctx.enter_context(nc.semaphore(name))

        PS = ctx.enter_context(nc.psum_tensor("PS", [P, 8, 512], F32))

        ident = sb("ident", [P, P])
        identb = sb("identb", [P, P], BF16)
        gt = sb("gt", [P, G8])
        iota3 = sb("iota3", [P, 3])
        iota8 = sb("iota8", [P, NE])
        ones = sb("ones", [1, P])
        onesb = sb("onesb", [96, P], BF16)
        REG = (T + 2 * HALO) * 2 * ND * D
        reg = sb("reg", [P, REG])
        onehot = reg[:, 0:NLEAF * 2 * TXT // 2].bitcast(BF16).rearrange("p (l n) -> p l n", n=TXT)
        uv = reg[:, :].rearrange("p (t n) -> p t n", n=2 * ND * D)
        img = sb("img", [P, B, IMG])
        onehot_op = img[:, :, :].rearrange("p b w -> p (b w)")[:, 0:NOP * TXT // 2]\
            .bitcast(BF16).rearrange("p (l n) -> p l n", n=TXT)
        imgf = img[:, :, :].rearrange("p b w -> p (b w)")
        taken = [0]

        def late(*shape):
            n = int(np.prod(shape))
            v = imgf[:, taken[0]:taken[0] + n]
            taken[0] += n
            names = "abc"[:len(shape)]
            return v.rearrange(f"p ({' '.join(names)}) -> p {' '.join(names)}", **dict(zip(names, shape)))

        spare = reg[:, NLEAF * TXT:]
        o1 = spare[:, 0:G8 * B].rearrange("p (g b) -> p g b", b=B)
        ya = sb("ya", [P, T, 8])
        yt = sb("yt", [D, 6, P])
        wbd = sb("wbd", [D, 8, D])
        tok = sb("tok", [P, SP], I32)
        idg = sb("idg", [P, SP, NID], I32)
        idb = sb("idb", [P, SP, NID], BF16)
        idsT = spare[0:NID, G8 * B:G8 * B + TXT // 2].bitcast(BF16)
        mask = sb("mask", [P, SP])
        mbeta = spare[:, G8 * B + TXT // 2:G8 * B + TXT // 2 + SP * D].rearrange("p (s d) -> p s d", d=D)
        bcb = sb("bcb", [P, 3, VB], BF16)
        wall = sb("wall", [P, 4, D])
        wsum = sb("wsum", [P, 4])
        wg = sb("wg", [P, 3, D])
        opT = sb("opT", [D, D])
        comp = sb("comp", [P, 2, D])
        zc = sb("zc", [P, 2, D])
        zcT = sb("zcT", [D, 2, P])
        stc = sb("stc", [P, 2, 6])
        mvc = sb("mvc", [P, 2, 2])
        rc = sb("rc", [P, 2])
        tgc = sb("tgc", [P, 1])
        tbc = sb("tbc", [P, 1])
        tgr = sb("tgr", [P, D])
        tbr = sb("tbr", [P, D])
        tabr = sb("tabr", [P, 5 * D])
        tab = sb("tab", [P, 3, 5 * D], BF16)
        opab = sb("opab", [P, 2, D], BF16)
        x1s = sb("x1s", [P, 8, D])
        z1 = sb("z1", [P, 8, D])
        z2 = sb("z2", [P, 4, D])
        z1T = sb("z1T", [P, 4, P])
        z2T_ = sb("z2Tt", [P, 2, P])
        sq = sb("sq", [P, 14, D])
        ss = sb("ss", [P, 14])
        rt = sb("rt", [P, 14])
        fin = sb("fin", [P, 2, D])
        hall = sb("hall", [P, T, D])
        zall = sb("zall", [P, T + 2 * HALO, D])
        zs = late(CH, 2, D)
        zT = sb("zT", [P, CH, P], F32R)
        wqkvT = sb("wqkvT", [D, ND, 3, D])
        wproj = sb("wproj", [D, D])
        bproj = sb("bproj", [P, D])
        mv32 = sb("mv32", [P, 2 * ND * D])
        mvh = sb("mvh", [P, 2 * ND * D], F32R)
        mvl = sb("mvl", [P, 2 * ND * D], F32R)
        st1 = sb("st1", [P, CH, 6])
        mm1 = sb("mm1", [P, CH, 2])
        r1 = sb("r1", [P, CH])
        prod = late(CH * ND * KW * D)
        lg = sb("lg", [P, CH, ND * KW])
        ex = sb("ex", [P, CH, ND * KW])
        at = sb("at", [P, CH, ND * KW])
        mx = sb("mx", [P, CH * ND])
        sm = sb("sm", [P, CH * ND])
        rs = sb("rs", [P, CH * ND])
        st2 = sb("st2", [P, CH, 6])
        mm2 = sb("mm2", [P, CH, 2])
        r2 = sb("r2", [P, CH])
        z32 = late(CH, D)
        z2s = late(CH, 2, D)
        z2T = sb("z2T", [P, CH, P], F32R)
        w1 = sb("w1", [P, NE * HID])
        w1h = sb("w1h", [P, NE * HID], F32R)
        w1l = sb("w1l", [P, NE * HID], F32R)
        wr = sb("wr", [P, NE])
        wrh = sb("wrh", [P, NE], F32R)
        wrl = sb("wrl", [P, NE], F32R)
        fgc = sb("fgc", [P, 1])
        fbc = sb("fbc", [P, 1])
        brow = sb("brow", [1, NE])
        br = sb("br", [P, NE])
        b1 = sb("b1", [P, NE])
        w2 = sb("w2", [P, NE, D])
        b2x = sb("b2x", [96, NE * D])
        b2b = sb("b2b", [96, NE * D], BF16)
        b2p = sb("b2p", [96, NE * D], BF16)
        rl = sb("rl", [P, CH, NE])
        v8 = sb("v8", [P, CH, NE])
        i8 = sb("i8", [P, CH, NE], U32)
        i8f = sb("i8f", [P, CH, 2])
        dm = sb("dm", [P, CH])
        th = sb("th", [P, CH])
        tw = sb("tw", [P, CH, 2])
        se1 = sb("se1", [P, CH, NE])
        se2 = sb("se2", [P, CH, NE])
        wf = sb("wf", [P, CH, NE])
        hT = late(NHT, CH, P)
        ybuf = late(NE // 2, CH * 2 * D)
        ysum = late(CH * 2 * D)

        ld_const = sem("ld_const")
        ld_tok = sem("ld_tok")
        ld_txt = sem("ld_txt")
        ld_att = sem("ld_att")
        ld_ffn = sem("ld_ffn")
        ld_b2 = sem("ld_b2")
        ld_emb = sem("ld_emb")
        ld_img = [sem(f"ld_img{i}") for i in range(4)]
        gathered = sem("gathered")
        zeroed = sem("zeroed")
        consts = sem("consts")
        vec = sem("vec")
        wc_ready = sem("wc_ready")
        vc_ready = sem("vc_ready")
        rc_ready = sem("rc_ready")
        zc_ready = sem("zc_ready")
        zct_done = sem("zct_done")
        zct_saved = sem("zct_saved")
        tab_done = sem("tab_done")
        tab_ready = sem("tab_ready")
        mv_done = sem("mv_done")
        mv_ready = sem("mv_ready")
        bias_done = sem("bias_done")
        ffn_ready = sem("ffn_ready")
        o1_done = sem("o1_done")
        o1_saved = sem("o1_saved")
        y_done = sem("y_done")
        ya_ready = sem("ya_ready")
        yt_done = sem("yt_done")
        yt_saved = sem("yt_saved")
        emb_done = sem("emb_done")
        emb_saved = sem("emb_saved")
        idb_ready = sem("idb_ready")
        idT_done = sem("idT_done")
        idT_saved = sem("idT_saved")
        bc_done = sem("bc_done")
        bc_saved = sem("bc_saved")
        bc_used = sem("bc_used")
        mb_ready = sem("mb_ready")
        mask_ready = sem("mask_ready")
        x_done = [sem(f"x{n}_done") for n in (1, 2, 3)]
        x1_saved = sem("x1_saved")
        sq_done = [sem(f"sq{n}_done") for n in (1, 2, 3)]
        ss_done = [sem(f"ss{n}_done") for n in (1, 2, 3)]
        rt_done = [sem(f"rt{n}_done") for n in (1, 2, 3)]
        z_done = [sem(f"z{n}_done") for n in (1, 2, 3)]
        zt_done = [sem(f"zt{n}_done") for n in (1, 2)]
        zt_saved = [sem(f"zt{n}_saved") for n in (1, 2)]
        var1 = sem("var1")
        rstd1 = sem("rstd1")
        zs_ready = sem("zs_ready")
        ztp_done = sem("ztp_done")
        zT_ready = sem("zT_ready")
        uv_done = sem("uv_done")
        uv_saved = sem("uv_saved")
        halo_v = sem("halo_v")
        halo_zero = sem("halo_zero")
        hb_ready = sem("hb_ready")
        halo_z = sem("halo_z")
        sp_ready = sem("sp_ready")
        at_ready = sem("at_ready")
        ap_ready = sem("ap_ready")
        apl_ready = sem("apl_ready")
        av_done = sem("av_done")
        sm_ready = sem("sm_ready")
        ex_ready = sem("ex_ready")
        var2 = sem("var2")
        rstd2 = sem("rstd2")
        z2s_ready = sem("z2s_ready")
        z2tp_done = sem("z2tp_done")
        z2T_ready = sem("z2T_ready")
        lg_done = sem("lg_done")
        lg_used = sem("lg_used")
        dm_ready = sem("dm_ready")
        th_ready = sem("th_ready")
        wf_ready = sem("wf_ready")
        h_done = sem("h_done")
        h_saved = sem("h_saved")
        y2_done = sem("y2_done")
        y_saved = sem("y_saved")
        y_used = sem("y_used")
        ysum_done = sem("ysum_done")
        out_ready = sem("out_ready")
        stored = sem("stored")

        col = lambda n, start=0: bass.AP(tensor=x[n].tensor, offset=start, ap=[[1, D], [1, 1]])
        row = lambda n, parts: bass.AP(tensor=x[n].tensor, offset=0, ap=[[0, parts], [1, D]])

        block = ctx.enter_context(nc.Block())

        def apart(eng, s, value, addressed=False):
            if not isinstance(value, int):
                value = eng.snap(eng.to_reg(value))
            for _ in range(1 + addressed):
                eng.wait_ge(zeroed, 1)
            eng.wait_ge(s, value)

        def has(k, first, last):
            return not isinstance(k, int) or first <= k <= last

        def upto(k, n):
            return min(k + n, NCH) if isinstance(k, int) else k + n

        def window(n, buf, t0, i, first):
            d = DIL[i]
            return ap_of(buf[:, bass.ds(t0 + HALO - d, 1), first:first + 1], [[n, CH], [d * n, KW], [1, D]])

        def products(i):
            return ap_of(prod[:, CH * KW * D * i:CH * KW * D * i + 1], [[KW * D, CH], [D, KW], [1, D]])

        def logit_products(eng, k, i):
            u = ap_of(uv[:, bass.ds(k * CH + HALO, 1), D * i:D * i + 1], [[2 * ND * D, CH], [0, KW], [1, D]])
            return eng.tensor_tensor(products(i), u, window(D, zall, k * CH, i, 0), ALU.mult)

        def value_products(eng, k, i):
            a = ap_of(at[:, 0:1, KW * i:KW * i + 1], [[ND * KW, CH], [1, KW], [0, D]])
            return eng.tensor_tensor(products(i), a, window(2 * ND * D, uv, k * CH, i, D * (ND + i)), ALU.mult)

        LOOP = (3, NCH - 3)

        def turns(eng, turn, count=None):
            for k in range(LOOP[0]):
                before = count.value() if count else 0
                turn(k)
            if count:
                per = count.value() - before
                count.enter(0, per)
                first = count.start
            with eng.Fori(*LOOP) as k:
                if count:
                    count.base = (k - LOOP[0]) * per + first
                turn(k)
            if count:
                count.leave(LOOP[1] - LOOP[0])
            for k in range(LOOP[1], NCH + 2):
                turn(k)

        LOG = CH * D

        def chunk_of(n):
            if isinstance(n, int):
                return NCH - 1 if n == 0 else n - 1
            return n - 1

        @block.sync
        def _(sp):
            sp.dma_start(tok[:, :], x["tok"]).then_inc(ld_tok, 16)
            sp.dma_start(ident[:, :], x["ident"]).then_inc(ld_const, 16)
            sp.dma_start(gt[:, :], x["gt"]).then_inc(ld_const, 16)
            sp.dma_start(iota3[:, :], x["iota3"]).then_inc(ld_const, 16)
            sp.dma_start(iota8[:, :], x["iota8"]).then_inc(ld_const, 16)
            for i in range(4):
                sp.dma_start(img[:, 16 * i:16 * i + 16, :], x["img"][:, 16 * i:16 * i + 16, :])\
                  .then_inc(ld_img[i], 16)
            sp.dma_start(w1[0:D, :], x["w1"]).then_inc(ld_ffn, 16)
            sp.dma_start(w1[D:P, :], x["w1"]).then_inc(ld_ffn, 16)
            sp.dma_start(w2[:, :, :], x["w2"]).then_inc(ld_ffn, 16)
            for h in range(2):
                sp.dma_start(wr[D * h:D * h + D, :], x["wr"]).then_inc(ld_ffn, 16)
                sp.dma_start(fgc[D * h:D * h + D, :], col("fg")).then_inc(ld_ffn, 16)
                sp.dma_start(fbc[D * h:D * h + D, :], col("fb")).then_inc(ld_ffn, 16)
            sp.dma_start(brow[:, :], x["br"].rearrange("(a n) -> a n", a=1)).then_inc(ld_ffn, 16)
            sp.dma_start(b1[:, :], x["b1"]).then_inc(ld_ffn, 16)
            sp.wait_ge(zeroed, 2)
            for q in range(3):
                sp.dma_start(b2x[32 * q:32 * q + 1, :], x["b2"].rearrange("(a n) -> a n", a=1))\
                  .then_inc(ld_b2, 16)
            o = x["out"].rearrange("b (h t) d -> h b t d", h=2)

            def store(k):
                sp.wait_ge(out_ready, k + 1)
                for h in range(2):
                    sp.dma_start(o[h, :, bass.ds(k * CH, CH), :],
                                 hall[D * h:D * h + D, bass.ds(k * CH, CH), :]).then_inc(stored, 16)

            with sp.Fori(0, NCH) as k:
                store(k)
            sp.wait_ge(stored, 16 * 2 * NCH)

        @block.gpsimd
        def _(pool):
            pool.wait_ge(ld_tok, 16)
            for s in range(SP):
                pool.indirect_dma_start(
                    out=idg[:, s, :], out_offset=None, in_=x["ids"],
                    in_offset=bass.IndirectOffsetOnAxis(ap=tok[:, s:s + 1].bitcast(U32), axis=0))\
                    .then_inc(gathered, 16)
            nh = sb("nh", [P, 16])
            pw = sem("pool_step")
            n_pw = Count(pw)

            t = n_pw.add(pool.memset(nh[:, :], -0.5))
            pool.wait_ge(pw, t)

            def root(out, var, scale, add, n, done):
                t = n_pw.add(pool.tensor_scalar(out, var, scale, add, ALU.mult, ALU.add))
                pool.wait_ge(pw, t)
                pool.tensor_tensor(out, out, nh[:, 0:n], ALU.pow).then_inc(done, 1)

            pool.wait_ge(vc_ready, 1)
            root(rc[:, :], mvc[:, :, 1], 1.0, EPS, 2, rc_ready)
            pool.wait_ge(mask_ready, 1)
            pool.wait_ge(ld_txt, TXT_LOADS * 16)
            pool.tensor_tensor(mbeta[:, :, :], mask[:, :].unsqueeze(2).to_broadcast([P, SP, D]),
                               tbr[:, :].unsqueeze(1).to_broadcast([P, SP, D]), ALU.mult).then_inc(mb_ready, 1)

            LV = ((0, 8), (8, 4), (12, 2))

            def text(g, lv):
                a, n = LV[lv]
                apart(pool, ss_done[lv], g - lv + 1)
                root(rt[:, a:a + n], ss[:, a:a + n], 1.0 / D, EPS, n, rt_done[lv])

            text(0, 0)
            text(1, 0)
            text(1, 1)
            n_pw.enter(0, 3)
            first = n_pw.start
            with pool.Fori(2, 8) as g:
                n_pw.base = (g - 2) * 3 + first
                for lv in range(3):
                    text(g, lv)
            n_pw.leave(6)
            text(8, 1)
            text(8, 2)
            text(9, 2)
            pool.wait_ge(x_done[0], 8)
            pool.wait_ge(z_done[2], 8)
            pool.memset(uv[0:D, 0:HALO, ND * D:], 0.0).then_inc(halo_zero, 1)
            pool.wait_ge(halo_zero, 1)
            pool.memset(uv[D:P, T + HALO:, ND * D:], 0.0).then_inc(halo_zero, 1)
            pool.wait_ge(halo_zero, 2)

            def norm1(n):
                apart(pool, var1, n + 1)
                root(r1[:, :], mm1[:, :, 1], 1.0, EPS, CH, rstd1)

            def bias(n):
                c = chunk_of(n)
                pool.wait_ge(zs_ready, n + 1)
                v = hall[:, bass.ds(c * CH, CH), :]
                pool.tensor_tensor(v, v, bproj[:, :].unsqueeze(1).to_broadcast([P, CH, D]), ALU.add)\
                    .then_inc(hb_ready, 1)

            def weighted(k):
                pool.wait_ge(wf_ready, k + 1)
                if not (isinstance(k, int) and k == 0):
                    pool.wait_ge(out_ready, k)
                for q in range(NE // 2):
                    pool.wait_ge(y_saved, k * (NE // 2) + q + 1)
                    y = ybuf[:, q, :]
                    w = ap_of(wf[:, 0:1, 2 * q:2 * q + 1], [[NE, CH], [1, 2], [0, D]])
                    split = lambda v: v.rearrange("p (t e d) -> p t e d", t=CH, e=2)
                    i = pool.tensor_tensor(split(ysum[:, :] if q == 0 else y), split(y), w, ALU.mult)
                    if q > 0:
                        pool.wait_ge(pw, n_pw.add(i))
                        i = pool.tensor_tensor(ysum[:, :], ysum[:, :], y, ALU.add)
                    i.then_inc(y_used, 1)
                    pool.wait_ge(y_used, k * (NE // 2) + q + 1)
                s4 = split(ysum[:, :])
                pool.tensor_tensor(s4[:, :, 0, :], s4[:, :, 0, :], s4[:, :, 1, :], ALU.add).then_inc(ysum_done, 1)

            def turn(k):
                if has(k, 0, NCH - 1):
                    if has(k, 1, NCH):
                        pool.wait_ge(av_done, k)
                    pool.wait_ge(uv_saved, upto(k, 2) * CH)
                    apart(pool, zs_ready, upto(k, 3), True)
                    logit_products(pool, k, ND - 1).then_inc(sp_ready, 1)
                if has(k, 2, NCH + 1):
                    weighted(k - 2)
                if has(k, 0, NCH - 4):
                    norm1(k + 3)
                if has(k, 0, NCH - 1):
                    pool.wait_ge(uv_saved, upto(k, 3) * CH)
                    apart(pool, at_ready, k + 1, True)
                    value_products(pool, k, ND - 1).then_inc(apl_ready, 1)
                if has(k, 0, NCH - 1):
                    apart(pool, var2, k + 1)
                    root(r2[:, :], mm2[:, :, 1], 1.0 + EPS, EPS2, CH, rstd2)
                if has(k, 0, NCH - 4):
                    bias(k + 3)

            pool.wait_ge(ld_att, ATT_LOADS * 16)
            for n in range(3):
                norm1(n)
                bias(n)
            pool.wait_ge(halo_z, 2)
            pool.wait_ge(halo_v, 1)
            turns(pool, turn, n_pw)

        @block.scalar
        def _(act):
            for h in range(2):
                act.dma_start(tgc[D * h:D * h + D, :], col("tg")).then_inc(ld_txt, 16)
                act.dma_start(tbc[D * h:D * h + D, :], col("tb")).then_inc(ld_txt, 16)
            act.dma_start(comp[:, :, :], x["comp"].rearrange("(c p) d -> p c d", p=P)).then_inc(ld_txt, 16)
            act.dma_start(opT[:, :], x["opT"]).then_inc(ld_txt, 16)
            act.wait_ge(zeroed, 1)
            act.dma_start(wall[:, 0, :], x["wbin"][D:3 * D, :]).then_inc(ld_txt, 16)
            act.dma_start(wall[0:D, 1, :], x["wbin"][0:D, :]).then_inc(ld_txt, 16)
            act.dma_start(wall[0:D, 2, :], x["wbin"][2 * D:3 * D, :]).then_inc(ld_txt, 16)
            act.dma_start(wall[0:1, 3, :], x["bbin"].rearrange("(a n) -> a n", a=1)).then_inc(ld_txt, 16)
            act.dma_start(tgr[:, :], row("tg", P)).then_inc(ld_txt, 16)
            act.dma_start(tbr[:, :], row("tb", P)).then_inc(ld_txt, 16)
            act.dma_start(wqkvT[:, :, :, :], x["wqkvT"]).then_inc(ld_att, 16)
            act.dma_start(wproj[:, :], x["wproj"]).then_inc(ld_att, 16)
            act.dma_start(bproj[:, :], row("bproj", P)).then_inc(ld_att, 16)
            act.wait_ge(zeroed, 3)
            for j in range(8):
                act.dma_start(wbd[8 * j:8 * j + 8, j, :], x["wemb"]).then_inc(ld_emb, 16)

            def save_o1(q):
                act.wait_ge(o1_done, q + 1)
                act.copy(o1[:, :, 16 * q:16 * q + 16].rearrange("p g b -> p b g"),
                         PS[:, q, :].rearrange("p (b g) -> p b g", b=16)).then_inc(o1_saved, 1)

            for q in range(3):
                save_o1(q)
            act.wait_ge(zct_done, 1)
            act.copy(zcT[:, :, :], PS[0:D, 6, 0:2 * P].rearrange("p (c n) -> p c n", c=2)).then_inc(zct_saved, 1)
            save_o1(3)
            for q in range(4):
                act.wait_ge(idT_done, q + 1)
                act.copy(idsT[:, 512 * q:512 * q + 512],
                         PS[0:NID, q % 2, 0:256].bitcast(BF16)).then_inc(idT_saved, 1)

            for q, i0, n, w in ((0, 0, 2, P), (0, 2, 2, D), (1, 4, 2, D)):
                act.wait_ge(yt_done, q + 1)
                c = (i0 % 4) * P
                act.copy(yt[:, i0:i0 + n, 0:w],
                         PS[0:D, 6 + q, c:c + n * P].rearrange("p (i n) -> p i n", i=n)[:, :, 0:w]).then_inc(yt_saved, 1)
            def save_tokens(i):
                act.wait_ge(emb_done, i + 1)
                parts = P if i < 2 else D
                act.copy(hall[0:parts, 8 * i:8 * i + 8, :],
                         PS[0:parts, 3 + i % 3, :].rearrange("p (j d) -> p j d", d=D)).then_inc(emb_saved, 1)

            def spread(v):
                for r in range(NLEAF + NOP):
                    s = r % 3
                    act.wait_ge(bc_done, v * 15 + r + 1)
                    if not (isinstance(v, int) and r < 3):
                        act.wait_ge(bc_used, v * 15 + r - 2)
                    act.copy(bcb[:, s, :], PS[:, s, :]).then_inc(bc_saved, 1)
                    if isinstance(v, int) and r % 2 == 0 and 2 <= r <= 12:
                        save_tokens(r // 2 - 1)

            spread(0)
            with act.Fori(1, 4) as v:
                spread(v)

            def square(g, lv):
                a, n = ((0, 8), (8, 4), (12, 2))[lv]
                act.wait_ge(x_done[lv], g - lv + 1)
                if not (isinstance(g, int) and g - lv < 1):
                    act.wait_ge(ss_done[lv], g - lv)
                if lv == 0:
                    if not (isinstance(g, int) and g == 0):
                        act.wait_ge(z_done[0], g)
                    act.copy(x1s[:, :, :], PS[:, 4, :].rearrange("p (n d) -> p n d", d=D)).then_inc(x1_saved, 1)
                    act.wait_ge(x1_saved, g + 1)
                src = x1s[:, :, :].rearrange("p n d -> p (n d)") if lv == 0 else \
                    (PS[:, 5, 0:256] if lv == 1 else PS[:, 6, 0:128])
                act.activation(sq[:, a:a + n, :], src.rearrange("p (n d) -> p n d", d=D), ACT.Square)\
                    .then_inc(sq_done[lv], 1)

            def save_zt(g, lv):
                act.wait_ge(zt_done[lv], g - lv)
                if lv == 0:
                    act.copy(z1T[:, :, :], PS[:, 0, :].rearrange("p (n q) -> p n q", n=4)).then_inc(zt_saved[0], 1)
                else:
                    act.copy(z2T_[:, :, :], PS[:, 1, 0:256].rearrange("p (n q) -> p n q", n=2)).then_inc(zt_saved[1], 1)

            def text(g, do):
                if "t1" in do:
                    save_zt(g, 0)
                if "t2" in do:
                    save_zt(g, 1)
                for lv in range(3):
                    if f"x{lv}" in do:
                        square(g, lv)

            text(0, TEXT_STEPS[0])
            text(1, TEXT_STEPS[1])
            text(2, TEXT_ALL)
            with act.Fori(3, 8) as g:
                text(g, TEXT_ALL)
            text(8, TEXT_STEPS[8])
            text(9, TEXT_STEPS[9])

            def save_zT(n):
                act.wait_ge(ztp_done, n + 1)
                if not (isinstance(n, int) and n == 0):
                    act.wait_ge(uv_done, n * CH)
                act.copy(zT[:, :, :], PS[:, 0, :].rearrange("p (t n) -> p t n", t=CH)).then_inc(zT_ready, 1)

            def save_uv(n, some):
                for t in some:
                    act.wait_ge(uv_done, n * CH + t + 1)
                    act.copy(uv[:, bass.ds(chunk_of(n) * CH + HALO + t, 1), :],
                             PS[:, (1, 7)[t % 2], 0:2 * ND * D].unsqueeze(1)).then_inc(uv_saved, 1)

            def norm1(n):
                save_zT(n)
                save_uv(n, range(CH))

            def gelu(k, e):
                act.wait_ge(h_done, k * NE + e + 1)
                if not (isinstance(k, int) and k == 0 and e < NHT):
                    act.wait_ge(y2_done, k * NE + e - NHT + 1)
                act.activation(hT[:, e % NHT, :, :], PS[:, 2 + e % 2, :].rearrange("p (t n) -> p t n", t=CH),
                               ACT.Gelu, bias=b1[:, e:e + 1]).then_inc(h_saved, 1)

            def save_y(k, q):
                act.wait_ge(y2_done, k * NE + 2 * q + 2)
                if not (isinstance(k, int) and k == 0):
                    act.wait_ge(y_used, (k - 1) * (NE // 2) + q + 1)
                act.copy(ybuf[:, q, :], PS[:, 4 + q % 2, :]).then_inc(y_saved, 1)

            def turn(k):
                now, ex_, n1 = has(k, 0, NCH - 1), has(k, 1, NCH), has(k, 0, NCH - 4)
                if ex_:
                    gelu(k - 1, 0)
                    gelu(k - 1, 1)
                if has(k, 1, NCH - 3):
                    save_uv(k + 2, (2, 3))
                if ex_:
                    gelu(k - 1, 2)
                if now:
                    act.wait_ge(sm_ready, k + 1)
                    act.activation(ex[:, :, :], lg[:, :, :], ACT.Tanh, scale=0.5).then_inc(ex_ready, 1)
                if ex_:
                    gelu(k - 1, 3)
                    save_y(k - 1, 0)
                    act.wait_ge(dm_ready, k)
                    act.activation(th[:, :], dm[:, :], ACT.Tanh, scale=0.5).then_inc(th_ready, 1)
                    gelu(k - 1, 4)
                    save_y(k - 1, 1)
                    gelu(k - 1, 5)
                if n1:
                    save_zT(k + 3)
                    save_uv(k + 3, (0, 1))
                if ex_:
                    gelu(k - 1, 6)
                    save_y(k - 1, 2)
                    gelu(k - 1, 7)
                if now:
                    act.wait_ge(z2tp_done, k + 1)
                    act.copy(z2T[:, :, :], PS[:, 0, :].rearrange("p (t n) -> p t n", t=CH)).then_inc(z2T_ready, 1)
                if ex_:
                    save_y(k - 1, 3)

            norm1(0)
            v0 = ND * D
            act.wait_ge(uv_saved, CH)
            act.copy(uv[D:P, 0:HALO, v0:], uv[0:D, T:T + HALO, v0:])
            norm1(1)
            act.wait_ge(uv_saved, 2 * CH)
            act.copy(uv[0:D, T + HALO:, v0:], uv[D:P, HALO:2 * HALO, v0:]).then_inc(halo_v, 1)
            norm1(2)
            act.wait_ge(ffn_ready, 1)
            turns(act, turn)

        @block.tensor
        def _(pe):
            def mm(out, lhsT, rhs, start, stop):
                return pe.matmul(out, lhsT, rhs, start=start, stop=stop, skip_group_check=True)

            def rows_transformed(q):
                pe.wait_ge(ld_img[q], 16)
                for b in range(16):
                    i = mm(PS[:, q, G8 * b:G8 * b + G8], img[:, 16 * q + b, :], gt[:, :], True, True)
                i.then_inc(o1_done, 1)

            pe.wait_ge(ld_const, 64)
            pe.wait_ge(consts, 1)
            for q in range(3):
                rows_transformed(q)
            pe.wait_ge(zc_ready, 1)
            for c in range(2):
                i = pe.transpose(PS[0:D, 6, P * c:P * c + P], zc[:, c, :], ident[:, :])
            i.then_inc(zct_done, 1)
            pe.wait_ge(wc_ready, 1)
            pe.wait_ge(zct_saved, 1)
            pe.wait_ge(ld_txt, TXT_LOADS * 16)
            for c in range(2):
                mm(PS[:, 5, P * c:P * c + D], zcT[:, c, :], wg[0:D, 0, :], True, True)
                mm(PS[:, 5, P * c + D:P * c + P], zcT[:, c, :], wg[0:D, 2, :], True, True)
            for h in range(2):
                o = PS[D * h:D * h + D, 5, 4 * D:5 * D]
                mm(o, opT[:, :], wall[0:D, 1, :], True, False)
                mm(o, tbc[:, :].to_broadcast([P, D]), wall[:, 0, :], False, False)
                i = mm(o, ones[:, 0:D], wall[0:1, 3, :], False, True)
            i.then_inc(tab_done, 1)
            pe.wait_ge(ld_att, ATT_LOADS * 16)
            for i in range(ND):
                for h in range(2):
                    o = PS[D * h:D * h + D, 7, :]
                    mm(o[:, D * i:D * i + D], wqkvT[:, i, 0, :], wqkvT[:, i, 1, :], True, True)
                    last = mm(o[:, D * (ND + i):D * (ND + i) + D], wqkvT[:, i, 2, :], wproj[:, :], True, True)
            last.then_inc(mv_done, 1)

            rows_transformed(3)
            pe.wait_ge(o1_saved, 4)
            pe.wait_ge(tab_ready, 1)
            for g in range(NG):
                for r in range(8):
                    half, i8_ = (0, r) if r < 6 else (1, r - 6)
                    c = (i8_ % 4) * P + g * G8
                    i = mm(PS[D * half:D * half + D, 4 + i8_ // 4, c:c + G8], o1[:, 8 * g + r, :], gt[:, :], True, True)
            i.then_inc(y_done, 1)
            pe.wait_ge(idb_ready, 1)
            for q in range(4):
                if q >= 2:
                    pe.wait_ge(idT_saved, q - 1)
                for s in range(4):
                    i = pe.transpose(PS[0:NID, q % 2, 64 * s:64 * s + 64].bitcast(BF16), idb[:, 4 * q + s, :], identb[:, :])
                i.then_inc(idT_done, 1)
            pe.wait_ge(ya_ready, 1)
            pe.wait_ge(mv_ready, 1)
            for i in range(6):
                n = P if i < 2 else D
                q = i // 4
                c = (i % 4) * P
                last = pe.transpose(PS[0:D, 6 + q, c:c + n],
                                    ya[0:n, 8 * i:8 * i + 8, :].rearrange("p j m -> p (j m)"), ident[0:n, 0:n])
                if i in (3, 5):
                    last.then_inc(yt_done, 1)
            def embed(i):
                if i % 4 == 0:
                    pe.wait_ge(yt_saved, (2, 3)[i // 4])
                if i >= 3:
                    pe.wait_ge(emb_saved, i - 2)
                n = P if i < 2 else D
                mm(PS[0:n, 3 + i % 3, :], yt[:, i, 0:n], wbd[:, :, :].rearrange("p j d -> p (j d)"), True, True)\
                    .then_inc(emb_done, 1)

            def biases():
                pe.wait_ge(ld_ffn, FFN_LOADS * 16)
                for e in range(NE):
                    mm(PS[:, 7, e:e + 1], w1[0:D, HID * e:HID * e + HID], fbc[0:D, :], True, True)
                mm(PS[:, 7, NE:2 * NE], fbc[0:D, :].to_broadcast([D, P]), wr[0:D, :], True, False)
                mm(PS[:, 7, NE:2 * NE], ones[:, :], brow[:, :], False, True).then_inc(bias_done, 1)

            pe.wait_ge(ld_emb, 128)
            pe.wait_ge(idT_saved, 4)

            def spread(v):
                for r in range(NLEAF + NOP):
                    if not (isinstance(v, int) and r < 3):
                        apart(pe, bc_saved, v * 15 + r - 2, True)
                    mm(PS[:, r % 3, :], identb[0:NID, r:r + 1].to_broadcast([NID, P]),
                       idsT[:, bass.ds(v * VB, VB)], True, True).then_inc(bc_done, 1)
                    if isinstance(v, int) and r % 2 == 1:
                        if r < 12:
                            embed(r // 2)
                        else:
                            biases()

            spread(0)
            with pe.Fori(1, 4) as v:
                spread(v)

            def level1(g, nodes):
                for n in nodes:
                    s, k = divmod(n, 4)
                    tokens = bass.ds((g * 2 + s) * P, P)
                    o = PS[:, 4, D * n:D * n + D]
                    for side in range(2):
                        for c in range(2):
                            for part in range(3):
                                mm(o, onehot[:, 2 * (2 * k + side) + c, tokens],
                                   tab[:, part, P * c + D * side:P * c + D * side + D], side + c + part == 0, False)
                    for part in range(2):
                        i = mm(o, onehot_op[:, k, tokens], opab[:, part, :], False, part == 1)
                return i

            def text(g, do):
                if "x0" in do:
                    if not (isinstance(g, int) and g == 0):
                        pe.wait_ge(x1_saved, g)
                    level1(g, range(6))
                if "t1" in do:
                    pe.wait_ge(z_done[0], g)
                    for n in range(4):
                        i = pe.transpose(PS[:, 0, P * n:P * n + P],
                                         z1[:, 2 * n:2 * n + 2, :].rearrange("p n d -> p (n d)"), ident[:, :])
                    i.then_inc(zt_done[0], 1)
                if "t2" in do:
                    pe.wait_ge(z_done[1], g - 1)
                    for n in range(2):
                        i = pe.transpose(PS[:, 1, P * n:P * n + P],
                                         z2[:, 2 * n:2 * n + 2, :].rearrange("p n d -> p (n d)"), ident[:, :])
                    i.then_inc(zt_done[1], 1)
                if "x0" in do:
                    level1(g, (6, 7)).then_inc(x_done[0], 1)
                if "x1" in do:
                    pe.wait_ge(zt_saved[0], g)
                    for s in range(2):
                        for k in range(2):
                            n = 2 * s + k
                            o = PS[:, 5, D * n:D * n + D]
                            mm(o, z1T[:, n, :], wg[:, 0, :], True, False)
                            for part in range(2):
                                i = mm(o, onehot_op[:, 4 + k, bass.ds((g * 2 - 2 + s) * P, P)],
                                       opab[:, part, :], False, part == 1)
                    i.then_inc(x_done[1], 1)
                if "x2" in do:
                    pe.wait_ge(zt_saved[1], g - 1)
                    if not (isinstance(g, int) and g == 2):
                        pe.wait_ge(z_done[2], g - 2)
                    for s in range(2):
                        o = PS[:, 6, D * s:D * s + D]
                        mm(o, z2T_[:, s, :], wg[:, 0, :], True, False)
                        for part in range(2):
                            i = mm(o, onehot_op[:, 6, bass.ds((g * 2 - 4 + s) * P, P)], opab[:, part, :], False, part == 1)
                    i.then_inc(x_done[2], 1)

            pe.wait_ge(bc_used, 60)
            text(0, TEXT_STEPS[0])
            text(1, TEXT_STEPS[1])
            text(2, TEXT_ALL)
            with pe.Fori(3, 8) as g:
                text(g, TEXT_ALL)
            text(8, TEXT_STEPS[8])
            text(9, TEXT_STEPS[9])

            def transpose1(n):
                pe.wait_ge(zs_ready, n + 1)
                if not (isinstance(n, int) and n < 4):
                    pe.wait_ge(z2T_ready, n - 3)
                for t in range(CH):
                    i = pe.transpose(PS[:, 0, P * t:P * t + P], zs[:, t, :, :].rearrange("p a d -> p (a d)"), ident[:, :])
                i.then_inc(ztp_done, 1)

            def project(n, some):
                pe.wait_ge(zT_ready, n + 1)
                for t in some:
                    if not (isinstance(n, int) and n == 0 and t < 2):
                        pe.wait_ge(uv_saved, n * CH + t - 1)
                    o = PS[:, (1, 7)[t % 2], 0:2 * ND * D]
                    mm(o, zT[:, t, :], mvh[:, :], True, False)
                    mm(o, zT[:, t, :], mvl[:, :], False, True).then_inc(uv_done, 1)

            def transpose2(k):
                pe.wait_ge(z2s_ready, k + 1)
                for t in range(CH):
                    i = pe.transpose(PS[:, 0, P * t:P * t + P], z2s[:, t, :, :].rearrange("p a d -> p (a d)"), ident[:, :])
                i.then_inc(z2tp_done, 1)

            def logits(k):
                if not (isinstance(k, int) and k == 0):
                    pe.wait_ge(lg_used, k)
                for t in range(CH):
                    o = PS[:, 6, LOG + NE * t:LOG + NE * t + NE]
                    mm(o, z2T[:, t, :], wrh[:, :], True, False)
                    i = mm(o, z2T[:, t, :], wrl[:, :], False, True)
                i.then_inc(lg_done, 1)

            def hidden(k, e):
                o = PS[:, 2 + e % 2, :]
                z = z2T[:, :, :].rearrange("p t n -> p (t n)")
                if e < 2 and not (isinstance(k, int) and k == 0):
                    pe.wait_ge(h_saved, k * NE + e - 1)
                mm(o, w1h[:, HID * e:HID * e + HID], z, True, False)
                mm(o, w1l[:, HID * e:HID * e + HID], z, False, True).then_inc(h_done, 1)

            def expert(k, e):
                q = e // 2
                pe.wait_ge(h_saved, k * NE + e + 1)
                if e + 2 < NE:
                    hidden(k, e + 2)
                if e % 2 == 0:
                    if not (isinstance(k, int) and k == 0 and q < 2):
                        pe.wait_ge(y_saved, k * (NE // 2) + q - 1)
                    mm(PS[:, 4 + q % 2, :], onesb[:, :],
                       b2p[:, 2 * D * q:2 * D * q + 2 * D].unsqueeze(1).to_broadcast([96, CH, 2 * D]), True, False)
                for t in range(CH):
                    c = (2 * t + e % 2) * D
                    i = mm(PS[:, 4 + q % 2, c:c + D], hT[:, e % NHT, t, :], w2[:, e, :], False, e % 2 == 1)
                i.then_inc(y2_done, 1)

            def add_values(k):
                o = PS[:, 6, 0:CH * D].rearrange("p (t d) -> p t d", d=D)
                for i in range(ND):
                    if i < ND - 1:
                        pe.wait_ge(ap_ready, k * (ND - 1) + i + 1)
                    else:
                        pe.wait_ge(apl_ready, k + 1)
                    for j in range(KW):
                        v = products(i).rearrange("p t k d -> p k t d")[:, j, :, :]
                        last = mm(o, ident[:, :], v, i + j == 0, i == ND - 1 and j == KW - 1)
                last.then_inc(av_done, 1)

            def turn(k):
                now, ex_, n1 = has(k, 0, NCH - 1), has(k, 1, NCH), has(k, 0, NCH - 4)
                if ex_:
                    pe.wait_ge(z2T_ready, k)
                    hidden(k - 1, 0)
                    hidden(k - 1, 1)
                if has(k, 1, NCH - 3):
                    project(k + 2, (2, 3))
                if ex_:
                    logits(k - 1)
                    for e in range(4):
                        expert(k - 1, e)
                if now:
                    add_values(k)
                if n1:
                    transpose1(k + 3)
                    project(k + 3, (0, 1))
                if ex_:
                    for e in range(4, 7):
                        expert(k - 1, e)
                if now:
                    transpose2(k)
                if ex_:
                    expert(k - 1, 7)

            pe.wait_ge(mv_ready, 1)
            for n in range(3):
                transpose1(n)
                project(n, range(CH))
            pe.wait_ge(ffn_ready, 1)
            turns(pe, turn)

        @block.vector
        def _(dve):
            own = Count(vec)

            def after(t, bare=False, addressed=False):
                (apart(dve, vec, t, addressed) if bare else dve.wait_ge(vec, t))

            dve.memset(wall[:, :, :], 0.0).then_inc(zeroed, 1)
            dve.memset(b2x[:, :], 0.0).then_inc(zeroed, 1)
            dve.memset(wbd[:, :, :], 0.0).then_inc(zeroed, 1)
            dve.memset(ones[:, :], 1.0)
            dve.memset(onesb[:, :], 1.0)
            own.add(dve.memset(opab[D:P, 1, :], 0.0))
            own.add(dve.memset(b2p[:, :], 0.0))
            own.add(dve.memset(ya[:, :, 7:8], 1.0))
            own.add(dve.memset(zall[0:D, 0:HALO, :], 0.0))
            own.add(dve.memset(zall[D:P, T + HALO:, :], 0.0))
            dve.wait_ge(ld_const, 64)
            dve.tensor_copy(identb[:, :], ident[:, :]).then_inc(consts, 1)

            dve.wait_ge(ld_txt, TXT_LOADS * 16)
            for c in range(2):
                t = own.add(dve.bn_stats(stc[:, c, :], comp[:, c, :]))
            after(t)
            for c in range(2):
                i = dve.bn_aggr(mvc[:, c, :], stc[:, c, :])
            i.then_inc(vc_ready, 1)
            t = own.add(dve.tensor_reduce(wsum[:, :], wall[:, :, :], AX.X, ALU.add))
            after(t)
            t = own.add(dve.tensor_scalar(wsum[:, :], wsum[:, :], 1.0 / D, None, ALU.mult))
            after(t)
            t = own.add(dve.tensor_tensor(wall[:, :, :], wall[:, :, :],
                                          wsum[:, :].unsqueeze(2).to_broadcast([P, 4, D]), ALU.subtract))
            after(t)
            for s in (0, 2):
                i = dve.tensor_scalar(wg[:, s, :], wall[:, s, :], tgc[:, 0:1], None, ALU.mult)
            i.then_inc(wc_ready, 1)
            dve.wait_ge(rc_ready, 1)
            for c in range(2):
                i = dve.tensor_scalar(zc[:, c, :], comp[:, c, :], mvc[:, c, 0:1], rc[:, c:c + 1],
                                      ALU.subtract, ALU.mult)
            i.then_inc(zc_ready, 1)
            dve.wait_ge(tab_done, 1)
            src = PS[:, 5, 0:5 * D]
            t = own.add(dve.tensor_copy(tab[:, 0, :], src))
            after(t)
            t = own.add(dve.tensor_tensor(tabr[:, :], src, tab[:, 0, :], ALU.subtract))
            after(t)
            t = own.add(dve.tensor_copy(tab[:, 1, :], tabr[:, :]))
            after(t)
            t = own.add(dve.tensor_tensor(tabr[:, :], tabr[:, :], tab[:, 1, :], ALU.subtract))
            after(t)
            t = own.add(dve.tensor_copy(tab[:, 2, :], tabr[:, :]))
            after(t)
            dve.tensor_copy(opab[0:D, 0, :], tab[0:D, 0, 4 * D:])
            dve.tensor_copy(opab[D:P, 0, :], tab[D:P, 1, 4 * D:])
            dve.tensor_copy(opab[0:D, 1, :], tab[0:D, 2, 4 * D:]).then_inc(tab_ready, 1)
            dve.wait_ge(mv_done, 1)
            nu = ND * D
            own.add(dve.tensor_scalar(mv32[:, 0:nu], PS[:, 7, 0:nu], float(D) ** -0.5, None, ALU.mult))
            t = own.add(dve.tensor_scalar(mv32[:, nu:], PS[:, 7, nu:2 * nu], 1.0 / ND, None, ALU.mult))
            after(t)
            t = own.add(dve.tensor_copy(mvh[:, :], mv32[:, :]))
            after(t)
            dve.tensor_tensor(mvl[:, :], mv32[:, :], mvh[:, :].bitcast(F32), ALU.subtract).then_inc(mv_ready, 1)

            t = own.add(dve.tensor_copy(mask[:, :], tok[:, :]))
            after(t)
            dve.tensor_scalar(mask[:, :], mask[:, :], 1.0, None, ALU.is_gt).then_inc(mask_ready, 1)

            dve.wait_ge(gathered, 16 * SP)
            dve.tensor_copy(idb[:, :, :], idg[:, :, :]).then_inc(idb_ready, 1)

            dve.wait_ge(ld_ffn, FFN_LOADS * 16)
            dve.wait_ge(ld_b2, 48)
            own.add(dve.tensor_scalar(w1h[:, :], w1[:, :], fgc[:, 0:1], None, ALU.mult))
            own.add(dve.tensor_scalar(wrh[:, :], wr[:, :], fgc[:, 0:1], None, ALU.mult))
            t = own.add(dve.tensor_copy(b2b[:, :], b2x[:, :]))
            after(t)
            dve.scalar_tensor_tensor(w1l[:, :], w1[:, :], fgc[:, 0:1], w1h[:, :].bitcast(F32), ALU.mult, ALU.subtract)
            dve.scalar_tensor_tensor(wrl[:, :], wr[:, :], fgc[:, 0:1], wrh[:, :].bitcast(F32), ALU.mult, ALU.subtract)
            own.add(dve.tensor_copy(b2p[0:1, :], b2b[0:1, :]))
            t = own.add(dve.tensor_tensor(b2x[:, :], b2x[:, :], b2b[:, :], ALU.subtract))
            after(t)
            t = own.add(dve.tensor_copy(b2b[:, :], b2x[:, :]))
            after(t)
            own.add(dve.tensor_copy(b2p[32:33, :], b2b[32:33, :]))
            t = own.add(dve.tensor_tensor(b2x[:, :], b2x[:, :], b2b[:, :], ALU.subtract))
            after(t)
            dve.tensor_copy(b2p[64:65, :], b2x[64:65, :])
            dve.wait_ge(y_done, 1)
            y = PS[:, 4:6, :].rearrange("p a n -> p (a n)")
            for n, half in ((6, 0), (2, 1)):
                p0 = D * half
                for g2 in range(2):
                    dst = bass.AP(tensor=ya[:, :, :].tensor, offset=ya[p0:p0 + D, 0:1, 2 * g2:2 * g2 + 1].offset,
                                  ap=[[T * 8, D], [64, n], [1, 2], [8, 8]])
                    s = y[p0:p0 + D, 0:n * P].rearrange("p (i g h j) -> p i g h j", i=n, g=NG, h=NG)
                    dve.tensor_copy(dst, s[:, :, 0:2, g2, :])
                for m, (g, g2) in ((4, (3, 2)), (5, (2, 3)), (6, (3, 3))):
                    dst = bass.AP(tensor=ya[:, :, :].tensor, offset=ya[p0:p0 + D, 0:1, m:m + 1].offset,
                                  ap=[[T * 8, D], [64, n], [8, 8]])
                    s = y[p0:p0 + D, 0:n * P].rearrange("p (i g h j) -> p i g h j", i=n, g=NG, h=NG)
                    i = dve.tensor_copy(dst, s[:, :, g, g2, :])
            i.then_inc(ya_ready, 1)

            def spread(v):
                for r in range(NLEAF + NOP):
                    s = r % 3
                    dve.wait_ge(bc_saved, v * 15 + r + 1)
                    if r < NLEAF:
                        for c in range(2):
                            i = dve.tensor_scalar(onehot[:, 2 * r + c, bass.ds(v * VB, VB)], bcb[:, s, :],
                                                  iota3[:, c:c + 1], None, ALU.is_equal)
                    else:
                        i = dve.tensor_scalar(onehot_op[:, r - NLEAF, bass.ds(v * VB, VB)], bcb[:, s, :],
                                              iota3[:, 2:3], None, ALU.is_equal)
                    i.then_inc(bc_used, 1)

            dve.wait_ge(o1_done, 4)
            with dve.Fori(0, 4) as v:
                spread(v)

            dve.wait_ge(bias_done, 1)
            own.add(dve.tensor_copy(br[:, :], PS[:, 7, NE:2 * NE]))
            dve.tensor_tensor(b1[:, :], b1[:, :], PS[:, 7, 0:NE], ALU.add).then_inc(ffn_ready, 1)

            dve.wait_ge(mb_ready, 1)
            LV = ((0, 8, 4), (8, 4, 5), (12, 2, 6))

            def sums(g, lv):
                a, n, _ = LV[lv]
                dve.wait_ge(sq_done[lv], g - lv + 1)
                dve.tensor_reduce(ss[:, a:a + n], sq[:, a:a + n, :], AX.X, ALU.add).then_inc(ss_done[lv], 1)

            def scaled(g, lv):
                a, n, bank = LV[lv]
                dve.wait_ge(rt_done[lv], g - lv + 1)
                src = x1s[:, :, :] if lv == 0 else PS[:, bank, 0:n * D].rearrange("p (n d) -> p n d", d=D)
                if lv < 2:
                    z = z1 if lv == 0 else z2
                    if not (isinstance(g, int) and g - lv < 1):
                        dve.wait_ge(zt_done[lv], g - lv)
                    dve.tensor_tensor(z[:, :, :], src, rt[:, a:a + n].unsqueeze(2).to_broadcast([P, n, D]), ALU.mult)\
                        .then_inc(z_done[lv], 1)
                    return
                pair = bass.ds(g * 2 - 4, 2)
                t = own.add(dve.tensor_tensor(rt[:, a:a + n], rt[:, a:a + n], mask[:, pair], ALU.mult))
                after(t)
                t = own.add(dve.tensor_tensor(fin[:, :, :], src, rt[:, a:a + n].unsqueeze(2).to_broadcast([P, n, D]), ALU.mult))
                after(t)
                t = own.add(dve.tensor_tensor(fin[:, :, :], fin[:, :, :], tgr[:, :].unsqueeze(1).to_broadcast([P, n, D]), ALU.mult))
                after(t)
                dst = hall[D:P, :, :].rearrange("p (t s) d -> p t s d", s=2)[:, bass.ds(g * 2 - 4 + TXT_T // 2, 2), :, :]
                for s in range(2):
                    i = dve.tensor_tensor(dst[:, :, s, :], fin[D * s:D * s + D, :, :], mbeta[D * s:D * s + D, pair, :], ALU.add)
                i.then_inc(z_done[2], 1)

            def text(g, do):
                for lv in range(3):
                    if f"x{lv}" in do:
                        sums(g, lv)
                for lv in range(3):
                    if f"x{lv}" in do:
                        scaled(g, lv)

            text(0, TEXT_STEPS[0])
            text(1, TEXT_STEPS[1])
            own.enter(0, 3)
            first = own.start
            with dve.Fori(2, 8) as g:
                own.base = (g - 2) * 3 + first
                text(g, TEXT_ALL)
            own.leave(6)
            text(8, TEXT_STEPS[8])
            text(9, TEXT_STEPS[9])

            def tiles(c):
                return bass.ds(c * CH, CH)

            def stats1(n):
                c = chunk_of(n)
                for t_ in range(CH):
                    t = own.add(dve.bn_stats(st1[:, t_, :], hall[:, bass.ds(c * CH + t_, 1), :].squeeze(1)))
                after(t, True)
                for t_ in range(CH):
                    i = dve.bn_aggr(mm1[:, t_, :], st1[:, t_, :])
                i.then_inc(var1, 1)

            def z1_(n):
                c = chunk_of(n)
                dve.wait_ge(rstd1, n + 1)
                if not (isinstance(n, int) and n == 0):
                    dve.wait_ge(ztp_done, n)
                for t_ in range(CH):
                    t = own.add(dve.tensor_scalar(zall[:, bass.ds(c * CH + t_ + HALO, 1), :].squeeze(1),
                                                  hall[:, bass.ds(c * CH + t_, 1), :].squeeze(1),
                                                  mm1[:, t_, 0:1], r1[:, t_:t_ + 1], ALU.subtract, ALU.mult))
                after(t, True, True)
                z = zall[:, bass.ds(c * CH + HALO, CH), :]
                t = own.add(dve.tensor_copy(zs[:, :, 0, :].bitcast(F32R), z))
                after(t)
                dve.tensor_tensor(zs[:, :, 1, :], z, zs[:, :, 0, :], ALU.subtract).then_inc(zs_ready, 1)

            def scores(k):
                dve.wait_ge(uv_saved, upto(k, 2) * CH)
                for i in range(ND):
                    if i < ND - 1:
                        after(own.add(logit_products(dve, k, i)))
                    else:
                        dve.wait_ge(sp_ready, k + 1)
                    t = own.add(dve.tensor_reduce(lg[:, :, KW * i:KW * i + KW], products(i), AX.X, ALU.add))
                after(t)
                l3 = lg[:, :, :].rearrange("p t (i k) -> p (t i) k", k=KW)
                t = own.add(dve.tensor_reduce(mx[:, :], l3, AX.X, ALU.max))
                after(t)
                dve.tensor_tensor(l3, l3, mx[:, :].unsqueeze(2).to_broadcast([P, CH * ND, KW]), ALU.subtract)\
                    .then_inc(sm_ready, 1)

            def attend(k):
                dve.wait_ge(ex_ready, k + 1)
                e3 = ex[:, :, :].rearrange("p t (i k) -> p (t i) k", k=KW)
                a3 = at[:, :, :].rearrange("p t (i k) -> p (t i) k", k=KW)
                t = own.add(dve.tensor_scalar(at[:, :, :], ex[:, :, :], -1.0, 1.0, ALU.mult, ALU.add))
                after(t)
                t = own.add(dve.reciprocal(at[:, :, :], at[:, :, :]))
                after(t)
                t = own.add(dve.scalar_tensor_tensor(ex[:, :, :], ex[:, :, :], 1.0, at[:, :, :], ALU.add, ALU.mult))
                after(t)
                t = own.add(dve.tensor_reduce(sm[:, :], e3, AX.X, ALU.add))
                after(t)
                t = own.add(dve.reciprocal(rs[:, :], sm[:, :]))
                after(t)
                dve.tensor_tensor(a3, e3, rs[:, :].unsqueeze(2).to_broadcast([P, CH * ND, KW]), ALU.mult)\
                    .then_inc(at_ready, 1)
                dve.wait_ge(at_ready, k + 1)
                dve.wait_ge(uv_saved, upto(k, 3) * CH)
                for i in range(ND - 1):
                    value_products(dve, k, i).then_inc(ap_ready, 1)

            def stats2(k):
                dve.wait_ge(hb_ready, upto(k, 2))
                dve.wait_ge(av_done, k + 1)
                h = hall[:, tiles(k), :]
                t = own.add(dve.tensor_tensor(h, h, PS[:, 6, 0:CH * D].rearrange("p (t d) -> p t d", d=D), ALU.add))
                after(t, True, True)
                for t_ in range(CH):
                    t = own.add(dve.bn_stats(st2[:, t_, :], hall[:, bass.ds(k * CH + t_, 1), :].squeeze(1)))
                after(t, True)
                for t_ in range(CH):
                    i = dve.bn_aggr(mm2[:, t_, :], st2[:, t_, :])
                i.then_inc(var2, 1)

            def z2_(k):
                dve.wait_ge(rstd2, k + 1)
                if not (isinstance(k, int) and k == 0):
                    dve.wait_ge(z2tp_done, k)
                for t_ in range(CH):
                    t = own.add(dve.tensor_scalar(z32[:, t_, :], hall[:, bass.ds(k * CH + t_, 1), :].squeeze(1),
                                                  mm2[:, t_, 0:1], r2[:, t_:t_ + 1], ALU.subtract, ALU.mult))
                after(t)
                t = own.add(dve.tensor_copy(z2s[:, :, 0, :].bitcast(F32R), z32[:, :, :]))
                after(t)
                dve.tensor_tensor(z2s[:, :, 1, :], z32[:, :, :], z2s[:, :, 0, :], ALU.subtract).then_inc(z2s_ready, 1)

            def top2(k):
                dve.wait_ge(lg_done, k + 1)
                dve.tensor_tensor(rl[:, :, :], PS[:, 6, LOG:LOG + CH * NE].rearrange("p (t e) -> p t e", e=NE),
                                  br[:, :].unsqueeze(1).to_broadcast([P, CH, NE]), ALU.add).then_inc(lg_used, 1)
                apart(dve, lg_used, k + 1)
                for t_ in range(CH):
                    t = own.add(dve.max(v8[:, t_, :], rl[:, t_, :]))
                after(t)
                dve.tensor_tensor(dm[:, :], v8[:, :, 1], v8[:, :, 0], ALU.subtract).then_inc(dm_ready, 1)

            def chosen():
                for t_ in range(CH):
                    t = own.add(dve.max_index(i8[:, t_, :], v8[:, t_, :], rl[:, t_, :]))
                after(t)
                t = own.add(dve.tensor_copy(i8f[:, :, :], i8[:, :, 0:2]))
                after(t)
                io = iota8[:, :].unsqueeze(1).to_broadcast([P, CH, NE])
                own.add(dve.tensor_tensor(se1[:, :, :], io, i8f[:, :, 0:1].to_broadcast([P, CH, NE]), ALU.is_equal))
                t = own.add(dve.tensor_tensor(se2[:, :, :], io, i8f[:, :, 1:2].to_broadcast([P, CH, NE]), ALU.is_equal))

            def weights(k):
                dve.wait_ge(th_ready, k + 1)
                own.add(dve.tensor_scalar(tw[:, :, 0], th[:, :], -0.5, 0.5, ALU.mult, ALU.add))
                t = own.add(dve.tensor_scalar(tw[:, :, 1], th[:, :], 0.5, 0.5, ALU.mult, ALU.add))
                after(t)
                own.add(dve.tensor_tensor(se1[:, :, :], se1[:, :, :], tw[:, :, 0:1].to_broadcast([P, CH, NE]), ALU.mult))
                t = own.add(dve.tensor_tensor(se2[:, :, :], se2[:, :, :], tw[:, :, 1:2].to_broadcast([P, CH, NE]), ALU.mult))
                after(t)
                if not (isinstance(k, int) and k == 0):
                    dve.wait_ge(y_used, k * (NE // 2))
                dve.tensor_tensor(wf[:, :, :], se1[:, :, :], se2[:, :, :], ALU.add).then_inc(wf_ready, 1)

            def combine(k):
                dve.wait_ge(ysum_done, k + 1)
                h = hall[:, tiles(k), :]
                dve.tensor_tensor(h, h, ysum[:, :].rearrange("p (t e d) -> p t e d", t=CH, e=2)[:, :, 0, :], ALU.add)\
                    .then_inc(out_ready, 1)

            dve.wait_ge(emb_saved, 6)
            dve.wait_ge(z_done[2], 8)
            stats1(0)
            z1_(0)
            dve.wait_ge(zs_ready, 1)
            dve.tensor_copy(zall[D:P, 0:HALO, :], zall[0:D, T:T + HALO, :]).then_inc(halo_z, 1)
            stats1(1)
            z1_(1)
            dve.wait_ge(zs_ready, 2)
            dve.tensor_copy(zall[0:D, T + HALO:, :], zall[D:P, HALO:2 * HALO, :]).then_inc(halo_z, 1)
            stats1(2)
            z1_(2)
            dve.wait_ge(zs_ready, 3)
            dve.wait_ge(halo_v, 1)
            dve.wait_ge(halo_zero, 2)
            dve.wait_ge(halo_z, 2)

            def turn(k):
                now, ex_ = has(k, 0, NCH - 1), has(k, 1, NCH)
                if now:
                    scores(k)
                if ex_:
                    top2(k - 1)
                if has(k, 0, NCH - 4):
                    stats1(k + 3)
                if now:
                    attend(k)
                if ex_:
                    chosen()
                if has(k, 0, NCH - 4):
                    z1_(k + 3)
                if now:
                    stats2(k)
                if has(k, 2, NCH + 1):
                    combine(k - 2)
                if ex_:
                    weights(k - 1)
                if now:
                    z2_(k)

            turns(dve, turn, own)


TXT_LOADS = 12
ATT_LOADS = 3
FFN_LOADS = 11
TEXT_ALL = ("t1", "t2", "x0", "x1", "x2")
TEXT_STEPS = {0: ("x0",), 1: ("t1", "x0", "x1"), 8: ("t1", "t2", "x1", "x2"), 9: ("t2", "x2")}


def operators():
    s = 0.7071067811865476

    def haar(n, sign):
        m = np.zeros((n // 2, n))
        m[np.arange(n // 2), 2 * np.arange(n // 2)] = s
        m[np.arange(n // 2), 2 * np.arange(n // 2) + 1] = sign * s
        return m

    def resize(n):
        f = n / 8
        at = (np.arange(8) + 0.5) * f - 0.5
        w = np.maximum(0, 1 - np.abs(at[:, None] - np.arange(n)[None, :]) / f)
        return w / w.sum(1, keepdims=True)

    lo, hi = haar(IMG, 1), haar(IMG, -1)
    rows = [resize(32) @ haar(64, 1) @ lo, resize(32) @ haar(64, -1) @ lo, resize(64) @ lo, resize(64) @ hi]
    return np.ascontiguousarray(np.concatenate(rows, 0).T.astype(np.float32))


def kernel(x, x_txt, L0_tok_W, L0_tok_b, L0_txt_leaf_ids, L0_txt_op_ids, L0_txt_comp_emb, L0_txt_op_emb,
           L0_txt_W_bin, L0_txt_b_bin, L0_txt_gamma, L0_txt_beta, L0_attn_Wqkv, L0_attn_Wproj, L0_attn_bproj,
           L0_ffn_gamma, L0_ffn_beta, L0_ffn_Wr, L0_ffn_br, L0_ffn_W1, L0_ffn_b1, L0_ffn_W2, L0_ffn_b2):
    import concourse.bacc as bacc
    from concourse.bass_utils import run_bass_kernel_spmd

    A = np.asarray
    cat = np.concatenate
    leaf, op = A(L0_txt_leaf_ids), A(L0_txt_op_ids)
    arrays = {
        "img": A(x)[:, 0].transpose(1, 0, 2),
        "tok": A(x_txt).reshape(B, SP, 2).transpose(2, 0, 1).reshape(P, SP),
        "ids": cat([leaf, op, np.zeros((leaf.shape[0], NID - NLEAF - NOP), leaf.dtype)], 1),
        "wemb": cat([A(L0_tok_W), A(L0_tok_b)[None, :]], 0),
        "comp": A(L0_txt_comp_emb), "opT": A(L0_txt_op_emb).T,
        "wbin": A(L0_txt_W_bin), "bbin": A(L0_txt_b_bin), "tg": A(L0_txt_gamma), "tb": A(L0_txt_beta),
        "wqkvT": A(L0_attn_Wqkv).reshape(ND, D, 3, D).transpose(3, 0, 2, 1),
        "wproj": A(L0_attn_Wproj), "bproj": A(L0_attn_bproj),
        "fg": A(L0_ffn_gamma), "fb": A(L0_ffn_beta), "wr": A(L0_ffn_Wr), "br": A(L0_ffn_br),
        "w1": A(L0_ffn_W1).transpose(1, 0, 2).reshape(D, NE * HID), "b1": A(L0_ffn_b1).T,
        "w2": A(L0_ffn_W2).transpose(1, 0, 2), "b2": A(L0_ffn_b2).reshape(-1),
        "ident": np.eye(P, dtype=np.float32), "gt": operators(),
        "iota3": np.stack([np.arange(P), np.arange(P) + P, np.arange(P) % D], 1).astype(np.float32),
        "iota8": np.tile(np.arange(NE, dtype=np.float32), (P, 1)),
    }
    arrays = {n: np.ascontiguousarray(a) for n, a in arrays.items()}
    nc = bacc.Bacc("TRN2", target_bir_lowering=False, num_devices=1)
    tensors = {n: nc.dram_tensor(f"in_{n}", a.shape, mybir.dt.from_np(a.dtype), kind="ExternalInput").ap()
               for n, a in arrays.items()}
    tensors["out"] = nc.dram_tensor("out_0", (B, NTOK, D), F32, kind="ExternalOutput").ap()
    build(nc, tensors)
    r = run_bass_kernel_spmd(nc, [{f"in_{n}": a for n, a in arrays.items()}], core_ids=[0])
    return r.results[0]["out_0"]
```
